# Optimizing a Trainium2 kernel written in Bass

```python
import numpy as np
import jax
import jax.numpy as jnp

def _softmax(x, axis=-1):
    return jax.nn.softmax(x, axis=axis)

def _gelu(x):
    return jax.nn.gelu(x, approximate=True)

def _silu(x):
    return jax.nn.silu(x)

def _sigmoid(x):
    return jax.nn.sigmoid(x)

def _layernorm(x, axis=-1, eps=1e-05):
    m = jnp.mean(x, axis=axis, keepdims=True)
    v = jnp.var(x, axis=axis, keepdims=True)
    return (x - m) / jnp.sqrt(v + eps)

def _scatter_add(tgt, idx, src, axis=0):
    return tgt.at[idx].add(src)

def _segment_sum(src, seg, n):
    return jax.ops.segment_sum(src, seg, n)
kernel_name = 'mk_adaln_d2_jaxref_r4_695829'

def setup_inputs(seed: int=0):
    np.random.seed(seed)
    _w = jnp.asarray

    def _L0_attn_setup():
        import jax, jax.numpy as jnp
        import numpy as np
        import math
        D_MODEL = 256
        N_HEADS = 16
        D_HEAD = D_MODEL // N_HEADS
        MAX_SEQ_LEN = 512
        BASE = 10000.0

        def _rope_tables(L):
            pos = jnp.arange(L, dtype=jnp.float32)[:, None]
            freqs = jnp.exp(-math.log(BASE) * jnp.arange(0, D_HEAD, 2, dtype=jnp.float32) / D_HEAD)
            angles = pos * freqs
            return (jnp.sin(angles), jnp.cos(angles))

        def _apply_rope(x, sin, cos):
            s = sin[None, :, None, :]
            c = cos[None, :, None, :]
            x_even, x_odd = (x[..., ::2], x[..., 1::2])
            rot_even = x_even * c - x_odd * s
            rot_odd = x_even * s + x_odd * c
            return jnp.stack([rot_even, rot_odd], axis=-1).reshape(x.shape)
        key = jax.random.key(seed)
        k0, k1, k2, k3, k4 = jax.random.split(key, 5)
        B, L = (2, 512)
        scale = 1.0 / math.sqrt(D_MODEL)
        return {'x': jax.random.normal(k0, (B, L, D_MODEL), dtype=jnp.float32), 'W_q': jax.random.normal(k1, (D_MODEL, D_MODEL), dtype=jnp.float32) * scale, 'W_k': jax.random.normal(k2, (D_MODEL, D_MODEL), dtype=jnp.float32) * scale, 'W_v': jax.random.normal(k3, (D_MODEL, D_MODEL), dtype=jnp.float32) * scale, 'W_o': jax.random.normal(k4, (D_MODEL, D_MODEL), dtype=jnp.float32) * scale}
    _L0_attn_in = _L0_attn_setup()

    def _L0_ffn_setup():
        import jax, jax.numpy as jnp
        import numpy as np
        E = 16
        K = 2
        LOAD = 1.0

        def _dispatch(xb, pb, cap):
            T, C = xb.shape
            top_k_probs, ei = jax.lax.top_k(pb, K)
            flat = ei.swapaxes(0, 1).ravel()
            one_hot = jax.nn.one_hot(flat, E, dtype=jnp.int32)
            pos = jnp.cumsum(one_hot, axis=0) * one_hot
            pos = pos.reshape(K, T, E).swapaxes(0, 1)
            pos = jnp.max(pos, axis=-1) - 1
            ei2 = flat.reshape(K, T).swapaxes(0, 1)
            xr = jnp.repeat(xb, K, axis=0)
            buf = jnp.zeros((E, cap, C), xb.dtype)
            buf = buf.at[ei2.ravel(), pos.ravel()].set(xr, mode='drop')
            return (top_k_probs, pos, ei2, buf)

        def _collect(eo_b, ei_b, pos_b, tk_b):
            out = eo_b[ei_b, pos_b]
            return jnp.sum(tk_b[..., None] * out, axis=1)
        key = jax.random.key(seed)
        k1, k2, k3, k4, k5 = jax.random.split(key, 5)
        B, T, C, H = (8, 1024, 256, 128)
        n_layer = 12
        x = jax.random.normal(k1, (B, T, C), dtype=jnp.float32)
        w_router = jax.random.normal(k2, (C, E), dtype=jnp.float32) * 0.02
        w_fc = jax.random.normal(k3, (E, C, H), dtype=jnp.float32) * 0.02
        w_gate = jax.random.normal(k4, (E, C, H), dtype=jnp.float32) * 0.02
        w_proj = jax.random.normal(k5, (E, H, C), dtype=jnp.float32) * (0.02 * (2 * n_layer) ** (-0.5))
        return {'x': x, 'w_router': w_router, 'w_fc': w_fc, 'w_gate': w_gate, 'w_proj': w_proj}
    _L0_ffn_in = _L0_ffn_setup()
    _L0_c = _w((lambda *s: np.random.randn(*s).astype(np.float32) * 0.05)(2, 256))
    _L0_wmod = _w((lambda *s: np.random.randn(*s).astype(np.float32) * 0.05)(256, 6 * 256) * 256 ** (-0.5))

    def _L1_attn_setup():
        import jax, jax.numpy as jnp
        import numpy as np
        D_MODEL = 256
        N_HEADS = 16
        HEAD_DIM = D_MODEL // N_HEADS
        EPS = 1e-06

        def _feature_map(t):
            return jax.nn.relu(t) + EPS
        key = jax.random.key(seed)
        ks = jax.random.split(key, 5)
        b, s = (2, 512)
        x = jax.random.normal(ks[0], (b, s, D_MODEL), dtype=jnp.float32)
        scale = 1.0 / np.sqrt(D_MODEL)
        Wq = jax.random.normal(ks[1], (D_MODEL, D_MODEL), dtype=jnp.float32) * scale
        Wk = jax.random.normal(ks[2], (D_MODEL, D_MODEL), dtype=jnp.float32) * scale
        Wv = jax.random.normal(ks[3], (D_MODEL, D_MODEL), dtype=jnp.float32) * scale
        Wo = jax.random.normal(ks[4], (D_MODEL, D_MODEL), dtype=jnp.float32) * scale
        return {'x': x, 'Wq': Wq, 'Wk': Wk, 'Wv': Wv, 'Wo': Wo}
    _L1_attn_in = _L1_attn_setup()

    def _L1_ffn_setup():
        import jax, jax.numpy as jnp
        import numpy as np
        NUM_HEADS = 16
        TOP_K = 2
        key = jax.random.key(seed)
        ks = jax.random.split(key, 5)
        B, S, D, E = (4, 512, 256, 8)
        scale = 0.02
        return {'x': jax.random.normal(ks[0], (B, S, D), dtype=jnp.float32), 'W_qkv': jax.random.normal(ks[1], (D, 3 * D), dtype=jnp.float32) * scale, 'b_qkv': jnp.zeros((3 * D,), dtype=jnp.float32), 'W_gate': jax.random.normal(ks[2], (D, E), dtype=jnp.float32) * scale, 'b_gate': jnp.zeros((E,), dtype=jnp.float32), 'W_experts': jax.random.normal(ks[3], (E, D, D), dtype=jnp.float32) * scale, 'b_experts': jnp.zeros((E, D), dtype=jnp.float32)}
    _L1_ffn_in = _L1_ffn_setup()
    _L1_c = _w((lambda *s: np.random.randn(*s).astype(np.float32) * 0.05)(2, 256))
    _L1_wmod = _w((lambda *s: np.random.randn(*s).astype(np.float32) * 0.05)(256, 6 * 256) * 256 ** (-0.5))
    _d = {'L0_attn_x': _L0_attn_in['x'], 'L0_attn_W_q': _L0_attn_in['W_q'], 'L0_attn_W_k': _L0_attn_in['W_k'], 'L0_attn_W_v': _L0_attn_in['W_v'], 'L0_attn_W_o': _L0_attn_in['W_o'], 'L0_ffn_w_router': _L0_ffn_in['w_router'], 'L0_ffn_w_fc': _L0_ffn_in['w_fc'], 'L0_ffn_w_gate': _L0_ffn_in['w_gate'], 'L0_ffn_w_proj': _L0_ffn_in['w_proj'], 'L0_c': _L0_c, 'L0_wmod': _L0_wmod, 'L1_attn_Wq': _L1_attn_in['Wq'], 'L1_attn_Wk': _L1_attn_in['Wk'], 'L1_attn_Wv': _L1_attn_in['Wv'], 'L1_attn_Wo': _L1_attn_in['Wo'], 'L1_ffn_W_qkv': _L1_ffn_in['W_qkv'], 'L1_ffn_b_qkv': _L1_ffn_in['b_qkv'], 'L1_ffn_W_gate': _L1_ffn_in['W_gate'], 'L1_ffn_b_gate': _L1_ffn_in['b_gate'], 'L1_ffn_W_experts': _L1_ffn_in['W_experts'], 'L1_ffn_b_experts': _L1_ffn_in['b_experts'], 'L1_c': _L1_c, 'L1_wmod': _L1_wmod}
    _x0 = _d['L0_attn_x']
    _d['L0_attn_x'] = jax.random.normal(jax.random.fold_in(jax.random.key(seed), 1), (2, 2048, 256), dtype=_x0.dtype)
    del _x0
    return _d

def reference(L0_attn_x, L0_attn_W_q, L0_attn_W_k, L0_attn_W_v, L0_attn_W_o, L0_ffn_w_router, L0_ffn_w_fc, L0_ffn_w_gate, L0_ffn_w_proj, L0_c, L0_wmod, L1_attn_Wq, L1_attn_Wk, L1_attn_Wv, L1_attn_Wo, L1_ffn_W_qkv, L1_ffn_b_qkv, L1_ffn_W_gate, L1_ffn_b_gate, L1_ffn_W_experts, L1_ffn_b_experts, L1_c, L1_wmod):

    def _L0_attn_ref(x, W_q, W_k, W_v, W_o):
        import jax, jax.numpy as jnp
        import numpy as np
        import math
        D_MODEL = 256
        N_HEADS = 16
        D_HEAD = D_MODEL // N_HEADS
        MAX_SEQ_LEN = 512
        BASE = 10000.0

        def _rope_tables(L):
            pos = jnp.arange(L, dtype=jnp.float32)[:, None]
            freqs = jnp.exp(-math.log(BASE) * jnp.arange(0, D_HEAD, 2, dtype=jnp.float32) / D_HEAD)
            angles = pos * freqs
            return (jnp.sin(angles), jnp.cos(angles))

        def _apply_rope(x, sin, cos):
            s = sin[None, :, None, :]
            c = cos[None, :, None, :]
            x_even, x_odd = (x[..., ::2], x[..., 1::2])
            rot_even = x_even * c - x_odd * s
            rot_odd = x_even * s + x_odd * c
            return jnp.stack([rot_even, rot_odd], axis=-1).reshape(x.shape)
        B, L, _ = x.shape
        sin, cos = _rope_tables(L)
        q = (x @ W_q.T).reshape(B, L, N_HEADS, D_HEAD)
        k = (x @ W_k.T).reshape(B, L, N_HEADS, D_HEAD)
        v = (x @ W_v.T).reshape(B, L, N_HEADS, D_HEAD)
        q = _apply_rope(q, sin, cos)
        k = _apply_rope(k, sin, cos)
        scores = jnp.einsum('blhd,bshd->bhls', q, k) / math.sqrt(D_HEAD)
        weights = jax.nn.softmax(scores, axis=-1)
        out = jnp.einsum('bhls,bshd->blhd', weights, v).reshape(B, L, D_MODEL)
        return out @ W_o.T

    def _L0_ffn_ref(x, w_router, w_fc, w_gate, w_proj):
        import jax, jax.numpy as jnp
        import numpy as np
        E = 16
        K = 2
        LOAD = 1.0

        def _dispatch(xb, pb, cap):
            T, C = xb.shape
            top_k_probs, ei = jax.lax.top_k(pb, K)
            flat = ei.swapaxes(0, 1).ravel()
            one_hot = jax.nn.one_hot(flat, E, dtype=jnp.int32)
            pos = jnp.cumsum(one_hot, axis=0) * one_hot
            pos = pos.reshape(K, T, E).swapaxes(0, 1)
            pos = jnp.max(pos, axis=-1) - 1
            ei2 = flat.reshape(K, T).swapaxes(0, 1)
            xr = jnp.repeat(xb, K, axis=0)
            buf = jnp.zeros((E, cap, C), xb.dtype)
            buf = buf.at[ei2.ravel(), pos.ravel()].set(xr, mode='drop')
            return (top_k_probs, pos, ei2, buf)

        def _collect(eo_b, ei_b, pos_b, tk_b):
            out = eo_b[ei_b, pos_b]
            return jnp.sum(tk_b[..., None] * out, axis=1)
        B, T, C = x.shape
        cap = int(LOAD * K * max(1, T / E))
        g = jnp.einsum('btc,ce->bte', x, w_router)
        gate_probs = jax.nn.softmax(g, axis=-1)
        top_k_probs, positions, indices, expert_inputs = jax.vmap(lambda xb, pb: _dispatch(xb, pb, cap))(x, gate_probs)
        expert_inputs = jnp.swapaxes(expert_inputs, 0, 1).reshape(E, B * cap, C)
        gg = jnp.einsum('enc,ech->enh', expert_inputs, w_gate)
        h = jnp.einsum('enc,ech->enh', expert_inputs, w_fc)
        h = jax.nn.silu(gg) * h
        o = jnp.einsum('enh,ehc->enc', h, w_proj)
        expert_outputs = jnp.swapaxes(o.reshape(E, B, cap, C), 0, 1)
        y = jax.vmap(_collect)(expert_outputs, indices, positions, top_k_probs)
        return y

    def _L1_attn_ref(x, Wq, Wk, Wv, Wo):
        import jax, jax.numpy as jnp
        import numpy as np
        D_MODEL = 256
        N_HEADS = 16
        HEAD_DIM = D_MODEL // N_HEADS
        EPS = 1e-06

        def _feature_map(t):
            return jax.nn.relu(t) + EPS
        b, s, _ = x.shape
        q = (x @ Wq.T).reshape(b, s, N_HEADS, HEAD_DIM)
        k = (x @ Wk.T).reshape(b, s, N_HEADS, HEAD_DIM)
        v = (x @ Wv.T).reshape(b, s, N_HEADS, HEAD_DIM)
        q = _feature_map(q).transpose(0, 2, 1, 3)
        k = _feature_map(k).transpose(0, 2, 1, 3)
        v = v.transpose(0, 2, 1, 3)
        kv = jnp.einsum('bhsd,bhsm->bhsdm', k, v)
        kv_cum = jnp.cumsum(kv, axis=2)
        out = jnp.einsum('bhsd,bhsdm->bhsm', q, kv_cum)
        k_cum = jnp.cumsum(k, axis=2)
        z = 1.0 / (jnp.einsum('bhsd,bhsd->bhs', q, k_cum) + EPS)
        out = out * z[..., None]
        out = out.transpose(0, 2, 1, 3).reshape(b, s, D_MODEL)
        return out @ Wo.T

    def _L1_ffn_ref(x, W_qkv, b_qkv, W_gate, b_gate, W_experts, b_experts):
        import jax, jax.numpy as jnp
        import numpy as np
        NUM_HEADS = 16
        TOP_K = 2
        B, S, D = x.shape
        H = NUM_HEADS
        hd = D // H
        E = W_gate.shape[-1]
        qkv = (x @ W_qkv + b_qkv).reshape(B, S, 3, H, hd)
        q, k, v = (qkv[:, :, 0], qkv[:, :, 1], qkv[:, :, 2])
        attn = jnp.einsum('bqhd,bkhd->bhqk', q, k) / jnp.sqrt(jnp.asarray(hd, x.dtype))
        attn = jax.nn.softmax(attn, axis=-1)
        attn_out = jnp.einsum('bhqk,bkhd->bqhd', attn, v).reshape(B, S, D)
        gate = jax.nn.softmax(x @ W_gate + b_gate, axis=-1)
        top_g, top_i = jax.lax.top_k(gate, TOP_K)
        combine = jnp.sum(jax.nn.one_hot(top_i, E, dtype=x.dtype) * top_g[..., None], axis=2)
        expert_out = jnp.einsum('bsd,edf->bsef', x, W_experts) + b_experts
        moe_out = jnp.einsum('bsef,bse->bsf', expert_out, combine)
        return attn_out + moe_out
    x = L0_attn_x
    mod = (_silu(L0_c) @ L0_wmod).reshape(L0_c.shape[0], 6, 1, -1)
    sa, ca, ga, sb, cb, gb = (mod[:, 0], mod[:, 1], mod[:, 2], mod[:, 3], mod[:, 4], mod[:, 5])
    ga = (2 * (ga >= 0) - 1) * jnp.maximum(jnp.abs(ga), 0.25)
    gb = (2 * (gb >= 0) - 1) * jnp.maximum(jnp.abs(gb), 0.25)
    h = _layernorm(x, axis=-1) * (1 + ca) + sa
    x = x + ga * _L0_attn_ref(h, L0_attn_W_q, L0_attn_W_k, L0_attn_W_v, L0_attn_W_o)
    h = _layernorm(x, axis=-1) * (1 + cb) + sb
    x = x + gb * _L0_ffn_ref(h, L0_ffn_w_router, L0_ffn_w_fc, L0_ffn_w_gate, L0_ffn_w_proj)
    mod = (_silu(L1_c) @ L1_wmod).reshape(L1_c.shape[0], 6, 1, -1)
    sa, ca, ga, sb, cb, gb = (mod[:, 0], mod[:, 1], mod[:, 2], mod[:, 3], mod[:, 4], mod[:, 5])
    ga = (2 * (ga >= 0) - 1) * jnp.maximum(jnp.abs(ga), 0.25)
    gb = (2 * (gb >= 0) - 1) * jnp.maximum(jnp.abs(gb), 0.25)
    h = _layernorm(x, axis=-1) * (1 + ca) + sa
    x = x + ga * _L1_attn_ref(h, L1_attn_Wq, L1_attn_Wk, L1_attn_Wv, L1_attn_Wo)
    h = _layernorm(x, axis=-1) * (1 + cb) + sb
    x = x + gb * _L1_ffn_ref(h, L1_ffn_W_qkv, L1_ffn_b_qkv, L1_ffn_W_gate, L1_ffn_b_gate, L1_ffn_W_experts, L1_ffn_b_experts)
    return x

_drawn_inputs = setup_inputs


def setup_inputs(seed=0):
    import zlib

    import numpy as np

    out = dict(_drawn_inputs(seed))
    spreads = {'L1_ffn_b_qkv': (0.0, 0.326), 'L1_ffn_b_gate': (0.0, 2.0), 'L1_ffn_b_experts': (0.0, 2.0)}
    factors = {'L0_attn_W_q': 4.815,
     'L0_attn_W_k': 4.28,
     'L0_attn_W_v': 3.967,
     'L0_attn_W_o': 3.992,
     'L0_ffn_w_router': 8.0,
     'L0_ffn_w_fc': 8.0,
     'L0_ffn_w_gate': 8.0,
     'L0_ffn_w_proj': 8.0,
     'L0_c': 3.857,
     'L0_wmod': 4.002,
     'L1_attn_Wq': 5.27,
     'L1_attn_Wk': 4.309,
     'L1_attn_Wv': 2.787,
     'L1_attn_Wo': 2.798,
     'L1_ffn_W_qkv': 8.0,
     'L1_ffn_W_gate': 3.119,
     'L1_ffn_W_experts': 2.787}
    for name, (base, spread) in spreads.items():
        noise = np.random.default_rng([zlib.crc32(name.encode()), seed]).standard_normal(out[name].shape)
        drawn = base * np.exp(spread * noise) if base else spread * noise
        out[name] = jnp.asarray(drawn.astype(out[name].dtype))
    for name, factor in factors.items():
        out[name] = (out[name] * factor).astype(out[name].dtype)
    return out
```

```python
from collections import namedtuple
from contextlib import ExitStack

import numpy as np

import concourse.bass as bass
from concourse import mybir

ALU = mybir.AluOpType
ACT = mybir.ActivationFunctionType
AX = mybir.AxisListType
F32 = mybir.dt.float32
BF16 = mybir.dt.bfloat16
I32 = mybir.dt.int32
U32 = mybir.dt.uint32
ds = bass.ds

P = 128
B, T, D = 2, 2048, 256
NH, HD = 16, 16
NT = B * T // P
TPB = T // P
G = 512
TPG = G // P
GPB = T // G
KH = D // P
HG = 4
NHG = NH // HG
AUG = HD + 1
VROW = HG * AUG
NPART = 3
QPART = (0, 0, 1, 0, 2, 1)
KPART = (0, 1, 0, 2, 0, 1)
SROWS = HD * len(QPART)
XROWS = SROWS + NPART
E0, CAP = 16, 256
SLOTS = E0 * B * CAP
E1 = 8
HID = 128
EPS_LN, EPS_LIN = 1e-5, 1e-6
HALF = D // 2
NHH = NH // KH


def named(**things):
    return namedtuple("Named", things)(**things)


def allocators(ctx, nc, tag):
    sems = []

    def semaphore(name):
        sems.append(nc.alloc_semaphore(f"{tag}_{name}"))
        return sems[-1]

    def clear():
        if sems:
            nc.clear_and_free_semaphores(sems)
            nc.all_engine_barrier()

    ctx.callback(clear)
    return (lambda name, shape, dt=F32: ctx.enter_context(nc.sbuf_tensor(f"{tag}_{name}", shape, dt)),
            lambda name, shape, dt=F32: ctx.enter_context(nc.psum_tensor(f"{tag}_{name}", shape, dt)),
            semaphore)


def settle(eng, m):
    eng.sem_inc(m.settled, 1)


def group_of(b, q):
    return b * GPB + q


def load_and_modulate(nc, m, io):
    with ExitStack() as ctx:
        sb, pb, sem = allocators(ctx, nc, "mod")
        wmod = sb("wmod", [P, 2, KH, 6 * D])
        cT = sb("cT", [P, 2, KH, B])
        sig = sb("sig", [P, 2, KH, B])
        cs = sb("cs", [P, 2 * KH * B])
        cs_rows = sb("cs_rows", [P, 2 * KH * B, P])
        gsign = sb("gsign", [P, 2, 2 * B * D])
        zeros = sb("zeros", [P, 2048])
        cols = pb("mod_cols", [P, 512])
        rows = pb("mod_rows", [P, 2 * B, 512])
        x_loaded, consts_loaded, c_loaded, w_loaded = sem("x_loaded"), sem("consts_loaded"), sem("c_loaded"), sem("w_loaded")
        c_exp, c_step, silu_ready, rows_ready = sem("c_exp"), sem("c_step"), sem("silu_ready"), sem("rows_ready")
        cols_done, gates_done, mod_step = sem("cols_done"), sem("gates_done"), sem("mod_step")
        zero_ready, slots_zeroed = sem("zero_ready"), sem("slots_zeroed")
        block = ctx.enter_context(nc.Block())

        @block.sync
        def _(sp):
            sp.dma_start(cT[:], io.c_t).then_inc(c_loaded, 16)
            sp.dma_start(wmod[:, 0], io.wmod[:, 0]).then_inc(w_loaded, 16)
            sp.dma_start(wmod[:, 1], io.wmod[:, 1]).then_inc(w_loaded, 16)
            xt = io.x.rearrange("(t p) d -> p t d", p=P)
            for b in range(B):
                sp.dma_start(m.x[:, b * TPB:(b + 1) * TPB], xt[:, b * TPB:(b + 1) * TPB]).then_inc(x_loaded, 16)
            sp.dma_start(m.ident[:], io.ident).then_inc(consts_loaded, 16)
            sp.dma_start(m.triu[:], io.triu).then_inc(consts_loaded, 16)
            sp.dma_start(m.iota[:], io.iota).then_inc(consts_loaded, 16)
            sp.wait_ge(zero_ready, 1)
            flat = io.slot_rows.rearrange("(p n) d -> p (n d)", p=P)
            for k in range(flat.shape[1] // 2048):
                sp.dma_start(flat[:, k * 2048:(k + 1) * 2048], zeros[:]).then_inc(slots_zeroed, 16)
            sp.wait_ge(x_loaded, 16 * B)
            sp.wait_ge(slots_zeroed, 16 * (flat.shape[1] // 2048))

        @block.gpsimd
        def _(pool):
            nc.gpsimd.memset(zeros[:], 0.0).then_inc(zero_ready, 1)

        @block.scalar
        def _(act):
            act.wait_ge(c_loaded, 16)
            nc.scalar.activation(sig[:], cT[:], ACT.Exp, scale=-1.0).then_inc(c_exp, 1)

        @block.tensor
        def _(pe):
            pe.wait_ge(silu_ready, 2)
            pe.wait_ge(w_loaded, 32)
            last = None
            for layer in range(2):
                for v, idx in enumerate((0, 1, 3, 4)):
                    for half in range(KH):
                        o = ((layer * 4 + v) * KH + half) * B
                        for kh in range(KH):
                            c0 = idx * D + half * P
                            k0 = (layer * KH + kh) * B
                            last = nc.tensor.matmul(cols[:, o:o + B], wmod[:, layer, kh, c0:c0 + P],
                                                    cs[:, k0:k0 + B], start=(kh == 0), stop=(kh == KH - 1))
            last.then_inc(cols_done, 1)
            for layer in range(2):
                for v, idx in enumerate((2, 5)):
                    for b in range(B):
                        o = b * D
                        for kh in range(KH):
                            last = nc.tensor.matmul(rows[:, layer * 2 + v, o:o + D],
                                                    cs_rows[:, (layer * KH + kh) * B + b, :],
                                                    wmod[:, layer, kh, idx * D:(idx + 1) * D],
                                                    start=(kh == 0), stop=(kh == KH - 1))
            last.then_inc(rows_ready, 1)

        @block.vector
        def _(dve):
            dve.wait_ge(c_exp, 1)
            sg = sig[:].rearrange("p a b c -> p (a b c)")
            nc.vector.tensor_scalar(sg, sg, 1.0, None, ALU.add).then_inc(c_step, 1)
            dve.wait_ge(c_step, 1)
            nc.vector.reciprocal(sg, sg).then_inc(c_step, 1)
            dve.wait_ge(c_step, 2)
            nc.vector.tensor_tensor(cs[:], sg, cT[:].rearrange("p a b c -> p (a b c)"), ALU.mult).then_inc(silu_ready, 1)
            dve.wait_ge(silu_ready, 1)
            nc.vector.tensor_copy(cs_rows[:], cs[:].unsqueeze(2).broadcast_to([P, 2 * KH * B, P])).then_inc(silu_ready, 1)
            dve.wait_ge(consts_loaded, 48)
            nc.vector.tensor_copy(m.ident_b[:], m.ident[:])
            nc.vector.tensor_copy(m.triu_b[:], m.triu[:])
            nc.vector.memset(m.eps[:], EPS_LN)
            dve.wait_ge(cols_done, 1)
            cv = cols[:, 0:16 * B].rearrange("p (l v r) -> p l v r", l=2, v=4)
            mv = m.modv[:].rearrange("p l v h b -> p l v (h b)")
            for v in (0, 2):
                nc.vector.tensor_copy(mv[:, :, v], cv[:, :, v])
                nc.vector.tensor_scalar(mv[:, :, v + 1], cv[:, :, v + 1], 1.0, None, ALU.add)
            dve.wait_ge(rows_ready, 1)
            for layer in range(2):
                rv = rows[:, layer * 2:layer * 2 + 2].rearrange("p a n -> p (a n)")
                gv = m.gates[:, layer].rearrange("p a b d -> p (a b d)")
                nc.vector.tensor_scalar(gsign[:, layer], rv, 0.0, 2.0, ALU.is_ge, ALU.mult).then_inc(mod_step, 1)
                dve.wait_ge(mod_step, 3 * layer + 1)
                nc.vector.tensor_scalar(gsign[:, layer], gsign[:, layer], -1.0, None, ALU.add).then_inc(mod_step, 1)
                dve.wait_ge(mod_step, 3 * layer + 2)
                nc.vector.tensor_tensor(gv, rv, gsign[:, layer], ALU.mult).then_inc(mod_step, 1)
                dve.wait_ge(mod_step, 3 * layer + 3)
                nc.vector.scalar_tensor_tensor(gv, gv, 0.25, gsign[:, layer], ALU.max, ALU.mult).then_inc(gates_done, 1)
            dve.wait_ge(gates_done, 2)


def ln_buffers(ctx, nc, tag):
    sb, pb, sem = allocators(ctx, nc, tag)
    return named(
        stats=sb("ln_stats", [P, TPG, 6]), mv=sb("ln_mv", [P, TPG, 2]), std=sb("ln_std", [P, TPG]),
        rstd=sb("ln_rstd", [P, TPG]), z=sb("ln_z", [P, TPG, D]), hT=sb("ln_hT", [P, KH, G]),
        zT=pb("ln_zT", [P, KH, G]),
        stats_done=sem("ln_stats_done"), var_ready=sem("ln_var_ready"), std_ready=sem("ln_std_ready"),
        rstd_ready=sem("ln_rstd_ready"), z_ready=sem("ln_z_ready"), zT_ready=sem("ln_zT_ready"),
        h_ready=sem("ln_h_ready"))


def ln_vector(nc, dve, m, ln, n, z_free, zT_free_at):
    settle(dve, m)
    for t in range(TPG):
        nc.vector.bn_stats(ln.stats[:, t], m.x[:, ds(n * TPG + t, 1)].rearrange("p a d -> p (a d)")).then_inc(ln.stats_done, 1)
    dve.wait_ge(ln.stats_done, n * TPG + TPG)
    settle(dve, m)
    for t in range(TPG):
        nc.vector.bn_aggr(ln.mv[:, t], ln.stats[:, t]).then_inc(ln.var_ready, 1)
    dve.wait_ge(ln.std_ready, n + 1)
    nc.vector.reciprocal(ln.rstd[:], ln.std[:]).then_inc(ln.rstd_ready, 1)
    dve.wait_ge(ln.rstd_ready, n + 1)
    dve.wait_ge(ln.zT_ready, n)
    z_free()
    for t in range(TPG):
        nc.vector.tensor_scalar(ln.z[:, t], m.x[:, ds(n * TPG + t, 1)].rearrange("p a d -> p (a d)"),
                                ln.mv[:, t, 0:1], ln.rstd[:, t:t + 1], ALU.subtract, ALU.mult).then_inc(ln.z_ready, 1)


def ln_tensor(nc, pe, m, ln, n):
    pe.wait_ge(ln.h_ready, n * KH)
    for t in range(TPG):
        pe.wait_ge(ln.z_ready, n * TPG + t + 1)
        for half in range(KH):
            last = nc.tensor.transpose(ln.zT[:, half, t * P:(t + 1) * P], ln.z[:, t, half * P:(half + 1) * P], m.ident[:])
    last.then_inc(ln.zT_ready, 1)


def ln_scalar(nc, act, m, ln, n, b, layer, which, hT_free):
    act.wait_ge(ln.var_ready, n * TPG + TPG)
    nc.scalar.activation(ln.std[:], ln.mv[:, :, 1], ACT.Sqrt, bias=m.eps[:, 0:1]).then_inc(ln.std_ready, 1)
    act.wait_ge(ln.zT_ready, n + 1)
    hT_free()
    for half in range(KH):
        shift = m.modv[:, layer, 2 * which, half, ds(b, 1)]
        scale = m.modv[:, layer, 2 * which + 1, half, ds(b, 1)]
        nc.scalar.activation(ln.hT[:, half], ln.zT[:, half], ACT.Identity, bias=shift, scale=scale).then_inc(ln.h_ready, 1)


def split_buffers(ctx, nc, tag):
    sb, pb, sem = allocators(ctx, nc, tag)
    return named(
        whole=sb("sp_whole", [P, 4, G]), rest=sb("sp_rest", [P, 4, G]), parts=sb("sp_parts", [P, 4, NPART, G], BF16),
        whole_ready=sem("sp_whole_ready"), hi_ready=sem("sp_hi_ready"), rest_ready=sem("sp_rest_ready"),
        mid_ready=sem("sp_mid_ready"), lo_ready=sem("sp_lo_ready"), stored=sem("sp_stored"))


def split_scalar_hi(nc, act, sp, n, a):
    act.wait_ge(sp.whole_ready, n * 4 + a + 1)
    act.wait_ge(sp.stored, n * (16 * 4 * NPART))
    nc.scalar.activation(sp.parts[:, a, 0], sp.whole[:, a], ACT.Copy).then_inc(sp.hi_ready, 1)


def split_vector_rest(nc, dve, sp, n, a):
    dve.wait_ge(sp.hi_ready, n * 4 + a + 1)
    nc.vector.tensor_tensor(sp.rest[:, a], sp.whole[:, a], sp.parts[:, a, 0], ALU.subtract).then_inc(sp.rest_ready, 1)


def split_scalar_mid(nc, act, sp, n, a):
    act.wait_ge(sp.rest_ready, n * 4 + a + 1)
    nc.scalar.activation(sp.parts[:, a, 1], sp.rest[:, a], ACT.Copy).then_inc(sp.mid_ready, 1)


def split_vector_lo(nc, dve, sp, n, a):
    dve.wait_ge(sp.mid_ready, n * 4 + a + 1)
    nc.vector.tensor_tensor(sp.parts[:, a, 2], sp.rest[:, a], sp.parts[:, a, 1], ALU.subtract).then_inc(sp.lo_ready, 1)


def split_store(sync, io, sp, n, b, q, paired):
    for a in range(4):
        sync.wait_ge(sp.lo_ready, n * 4 + a + 1)
        dram = (io.q_parts, io.k_parts)[a // 2]
        r = a % 2
        for part in range(NPART):
            rows = dram[part, ds(b, 1)].rearrange("a g h c t -> (a g h) c t")[:, :, ds(q * G, G)]
            if paired:
                dst = rows[:, r * (HD // 2):(r + 1) * (HD // 2)]
                src = sp.parts[:, a, part]
            else:
                dst = rows[r * NHH:(r + 1) * NHH].rearrange("h c t -> (h c) t")
                src = sp.parts[:, a, part]
            sync.dma_start(dst, src).then_inc(sp.stored, 16)


def store_values(sync, io, va, v_copied, v_stored, n, b, q):
    sync.wait_ge(v_copied, n * 2 + 2)
    for g in range(NHG):
        dst = io.v_rows[ds(b, 1), g].rearrange("a p t n -> (a p) t n")[:, ds(q * TPG, TPG)]
        sync.dma_start(dst, va[:, :, g * VROW:(g + 1) * VROW]).then_inc(v_stored, 16)


def project_layer0(nc, m, io):
    with ExitStack() as ctx:
        sb, pb, sem = allocators(ctx, nc, "qkv0")
        ln, sp = ln_buffers(ctx, nc, "qkv0"), split_buffers(ctx, nc, "qkv0")
        w_qk = sb("w_qk", [P, KH, 4 * P])
        w_v = sb("w_v", [P, KH, D])
        cos, sin = sb("cos", [P, T]), sb("sin", [P, T])
        prod = sb("prod", [P, 4, G])
        va = sb("va", [P, TPG, NH * AUG])
        qk_ps = pb("qk_ps", [P, 4, G])
        v_ps = pb("v_ps", [P, TPG, D])
        loaded, ones_set = sem("loaded"), sem("ones_set")
        qk_ready, v_ready, v_copied, v_stored = sem("qk_ready"), sem("v_ready"), sem("v_copied"), sem("v_stored")
        prod_ready = sem("prod_ready")
        block = ctx.enter_context(nc.Block())

        @block.sync
        def _(sync):
            sync.dma_start(w_qk[:], io.l0_wqk).then_inc(loaded, 16)
            sync.dma_start(w_v[:], io.l0_wv).then_inc(loaded, 16)
            sync.dma_start(cos[:], io.cos).then_inc(loaded, 16)
            sync.dma_start(sin[:], io.sin).then_inc(loaded, 16)
            with sync.Fori(0, B) as b:
                with sync.Fori(0, GPB) as q:
                    n = group_of(b, q)
                    store_values(sync, io, va, v_copied, v_stored, n, b, q)
                    split_store(sync, io, sp, n, b, q, paired=True)
            sync.wait_ge(v_stored, B * GPB * 16 * NHG)
            sync.wait_ge(sp.stored, B * GPB * 16 * 4 * NPART)

        @block.gpsimd
        def _(pool):
            nc.gpsimd.memset(va[:].rearrange("p t (h c) -> p (t h) c", c=AUG)[:, :, HD:AUG], 1.0).then_inc(ones_set, 1)

        @block.vector
        def _(dve):
            dve.wait_ge(loaded, 64)
            with dve.Fori(0, B) as b:
                with dve.Fori(0, GPB) as q:
                    n = group_of(b, q)
                    ln_vector(nc, dve, m, ln, n, lambda: None, None)
                    c, s = cos[:, ds(q * G, G)], sin[:, ds(q * G, G)]
                    for a in range(2):
                        dve.wait_ge(qk_ready, n * 4 + 2 * a + 2)
                        dve.wait_ge(sp.whole_ready, n * 4 + 2 * a)
                        for r, (src, by) in enumerate(((0, c), (1, s), (0, s), (1, c))):
                            nc.vector.tensor_tensor(prod[:, r], qk_ps[:, 2 * a + src], by, ALU.mult).then_inc(prod_ready, 1)
                        dve.wait_ge(prod_ready, n * 8 + 4 * a + 4)
                        dve.wait_ge(sp.lo_ready, n * 4)
                        nc.vector.tensor_tensor(sp.whole[:, 2 * a], prod[:, 0], prod[:, 1], ALU.subtract).then_inc(sp.whole_ready, 1)
                        nc.vector.tensor_tensor(sp.whole[:, 2 * a + 1], prod[:, 2], prod[:, 3], ALU.add).then_inc(sp.whole_ready, 1)
                    for a in range(4):
                        split_vector_rest(nc, dve, sp, n, a)
                    for a in range(4):
                        split_vector_lo(nc, dve, sp, n, a)

        @block.scalar
        def _(act):
            act.wait_ge(ones_set, 1)
            with act.Fori(0, B) as b:
                with act.Fori(0, GPB) as q:
                    n = group_of(b, q)
                    ln_scalar(nc, act, m, ln, n, b, 0, 0, lambda: act.wait_ge(v_ready, n * 2))
                    for a in range(2):
                        split_scalar_hi(nc, act, sp, n, a)
                    act.wait_ge(v_stored, n * (16 * NHG))
                    for pair in range(2):
                        act.wait_ge(v_ready, n * 2 + pair + 1)
                        dst = va[:, 2 * pair:2 * pair + 2].rearrange("p t (h c) -> p t h c", c=AUG)[:, :, :, 0:HD]
                        src = v_ps[:, 2 * pair:2 * pair + 2].rearrange("p t (h c) -> p t h c", c=HD)
                        nc.scalar.activation(dst, src, ACT.Copy).then_inc(v_copied, 1)
                    for a in range(2, 4):
                        split_scalar_hi(nc, act, sp, n, a)
                    for a in range(4):
                        split_scalar_mid(nc, act, sp, n, a)

        @block.tensor
        def _(pe):
            pe.wait_ge(loaded, 64)
            with pe.Fori(0, B) as b:
                with pe.Fori(0, GPB) as q:
                    n = group_of(b, q)
                    ln_tensor(nc, pe, m, ln, n)
                    pe.wait_ge(ln.h_ready, n * KH + KH)
                    pe.wait_ge(prod_ready, n * 8)
                    for a in range(4):
                        for kh in range(KH):
                            last = nc.tensor.matmul(qk_ps[:, a], w_qk[:, kh, a * P:(a + 1) * P], ln.hT[:, kh],
                                                    start=(kh == 0), stop=(kh == KH - 1))
                        last.then_inc(qk_ready, 1)
                    pe.wait_ge(v_copied, n * 2)
                    for t in range(TPG):
                        for kh in range(KH):
                            last = nc.tensor.matmul(v_ps[:, t], ln.hT[:, kh, t * P:(t + 1) * P], w_v[:, kh],
                                                    start=(kh == 0), stop=(kh == KH - 1))
                        if t % 2:
                            last.then_inc(v_ready, 1)


NB = GPB * 2
KT = TPB
TURN_AT = (12, 14)
COPY_AT = (12, 13, 14, 15)
LEAD = 7
MAXI = HG * TPG * 2


def softmax_attention(nc, m, io, tag):
    with ExitStack() as ctx:
        sb, pb, sem = allocators(ctx, nc, tag)
        QR = 4
        q_sb = sb("q_sb", [P, QR, HG, G], BF16)
        k_sb = sb("k_sb", [P, 2, HG, T], BF16)
        v_sb = sb("v_sb", [P, 2, TPB, VROW])
        probs = sb("probs", [P, 2, HG, G])
        part_max = sb("part_max", [P, 2, MAXI])
        row_max = sb("row_max", [P, HG * TPG])
        max_rest = sb("max_rest", [P, HG * TPG])
        max_parts = sb("max_parts", [P, HG * TPG, NPART], BF16)
        o_sb = sb("o_sb", [P, G])
        inv = sb("inv", [P, TPG, HG])
        s_ps = pb("s_ps", [P, 2, G])
        max_ps = pb("max_ps", [P, 2, 2, G])
        o_ps = pb("o_ps", [P, G])
        turn_ps = pb("turn_ps", [P, TPG, P])
        turn_b = turn_ps[:].rearrange("p a b -> p (a b)").bitcast(BF16)
        q_loaded = [sem(f"q_loaded{r}") for r in range(QR)]
        k_loaded = [sem(f"k_loaded{r}") for r in range(2)]
        v_loaded = [sem(f"v_loaded{r}") for r in range(2)]
        rows_set, o_zeroed = sem("rows_set"), sem("o_zeroed")
        s_ready, exp_done, pv_done = sem("s_ready"), sem("exp_done"), sem("pv_done")
        maxs_ready, max_taken = sem("maxs_ready"), sem("max_taken")
        rowmax_step, parts_ready, maxT_ready, maxT_copied = sem("rowmax_step"), sem("parts_ready"), sem("maxT_ready"), sem("maxT_copied")
        o_copied, turned, inv_ready, att_done = sem("o_copied"), sem("turned"), sem("inv_ready"), sem("att_done")
        NIT = B * NHG // 2
        att = m.att[:].rearrange("p b (i g) t n -> p (b i) g t n", g=2)
        kd = io.k_parts.rearrange("s b (i g) h c t -> s (b i) g c h t", g=2)
        qd = io.q_parts.rearrange("s b (i g) h c t -> s (b i) g c h t", g=2)
        vd = io.v_rows.rearrange("b (i g) p t n -> (b i) g p t n", g=2)
        block = ctx.enter_context(nc.Block())

        def load_q(eng, it, j):
            for r, part in enumerate(QPART):
                src = qd[part, ds(it, 1), j // GPB].rearrange("a c h t -> (a c) h t")
                eng.dma_start(q_sb[r * HD:(r + 1) * HD, j % QR],
                              src[:, :, (j % GPB) * G:(j % GPB + 1) * G]).then_inc(q_loaded[j % QR], 16)

        def load_k(eng, it, g):
            for r, part in enumerate(KPART):
                src = kd[part, ds(it, 1), g].rearrange("a c h t -> (a c) h t")
                eng.dma_start(k_sb[r * HD:(r + 1) * HD, g], src).then_inc(k_loaded[g], 16)

        def load_v(eng, it, g):
            eng.dma_start(v_sb[:, g], vd[ds(it, 1), g].rearrange("a p t n -> (a p) t n")).then_inc(v_loaded[g], 16)

        NQ, NK = 16 * len(QPART), 16 * len(KPART)

        @block.sync
        def _(sync):
            for j in range(3):
                load_q(sync, 0, j)
            load_k(sync, 0, 0)
            load_v(sync, 0, 0)
            with sync.Fori(0, NIT) as it:
                ahead = (it + 1) % NIT
                for j in range(NB):
                    n = it * NB + j
                    sync.wait_ge(exp_done, n * (KT * HG))
                    load_q(sync, it if j + 3 < NB else ahead, (j + 3) % NB)
                    if j % GPB == 0:
                        load_k(sync, it if j == 0 else ahead, 1 - j // GPB)
                        sync.wait_ge(pv_done, n * KT)
                        load_v(sync, it if j == 0 else ahead, 1 - j // GPB)
            for r in range(QR):
                sync.wait_ge(q_loaded[r], NQ * (B * NHG * GPB // QR + (r < 3)))
            for g in range(2):
                sync.wait_ge(k_loaded[g], NK * (NIT + (g == 0)))
                sync.wait_ge(v_loaded[g], 16 * (NIT + (g == 0)))

        @block.gpsimd
        def _(pool):
            nc.gpsimd.memset(k_sb[SROWS:XROWS], -1.0).then_inc(rows_set, 1)

        def max_scores(pe, n, j, k, it2):
            if k == 0:
                pe.wait_ge(q_loaded[j % QR], NQ * (it2 * (NB // QR) + j // QR + 1))
                if j % GPB == 0:
                    pe.wait_ge(k_loaded[j // GPB], NK * (it2 + 1))
            head, tile, half = k // (2 * TPG), k // 2 % TPG, k % 2
            if not (isinstance(n, int) and n * MAXI + k < 2):
                pe.wait_ge(max_taken, n * MAXI + k - 1)
            for c in range(2):
                last = nc.tensor.matmul(max_ps[:, k % 2, c], q_sb[0:SROWS, j % QR, head, tile * P:(tile + 1) * P],
                                        k_sb[0:SROWS, j // GPB, head, (2 * half + c) * G:(2 * half + c + 1) * G],
                                        start=True, stop=True)
                if c == 0:
                    yield
            last.then_inc(maxs_ready, 1)
            yield

        def max_take(dve, n, j, k):
            dve.wait_ge(maxs_ready, n * MAXI + k + 1)
            nc.vector.reduce_max(part_max[:, j % 2, k:k + 1], max_ps[:, k % 2].rearrange("p a n -> p (a n)"), AX.X).then_inc(max_taken, 1)

        def row_maxima(dve, n, j, s):
            if s == 0:
                dve.wait_ge(max_taken, (n + 1) * MAXI)
                nc.vector.reduce_max(row_max[:], part_max[:, j % 2].rearrange("p (a h) -> p a h", h=2), AX.X).then_inc(rowmax_step, 1)
            elif s == 1:
                dve.wait_ge(rowmax_step, n * 4 + 1)
                dve.wait_ge(maxT_ready, n * 2)
                nc.vector.tensor_copy(max_parts[:, :, 0], row_max[:]).then_inc(rowmax_step, 1)
            elif s == 2:
                dve.wait_ge(rowmax_step, n * 4 + 2)
                nc.vector.tensor_tensor(max_rest[:], row_max[:], max_parts[:, :, 0], ALU.subtract).then_inc(rowmax_step, 1)
            elif s == 3:
                dve.wait_ge(rowmax_step, n * 4 + 3)
                nc.vector.tensor_copy(max_parts[:, :, 1], max_rest[:]).then_inc(rowmax_step, 1)
            elif s == 4:
                dve.wait_ge(rowmax_step, n * 4 + 4)
                nc.vector.tensor_tensor(max_parts[:, :, 2], max_rest[:], max_parts[:, :, 1], ALU.subtract).then_inc(parts_ready, 1)

        def turn_maxima(pe, n, r):
            if r == 0:
                pe.wait_ge(parts_ready, n + 1)
                if not isinstance(n, int):
                    pe.wait_ge(att_done, n - 1)
            pe.wait_ge(maxT_copied, n * HG + 2 * r)
            for i in range(2 * TPG):
                last = nc.tensor.transpose(turn_b[SROWS:XROWS, i * P:(i + 1) * P],
                                           max_parts[:, r * 2 * TPG + i], m.ident_b[:])
            last.then_inc(maxT_ready, 1)

        def copy_maxima(act, n, j, h):
            act.wait_ge(maxT_ready, n * 2 + h // 2 + 1)
            nc.scalar.activation(q_sb[SROWS:XROWS, j % QR, h], turn_b[SROWS:XROWS, h % 2 * G:(h % 2 + 1) * G],
                                 ACT.Copy).then_inc(maxT_copied, 1)

        @block.tensor
        def _(pe):
            def items(n, j, ks, it2):
                for k in ks:
                    yield from max_scores(pe, n, j, k, it2)

            def scores(n, j, u, h):
                c = (n * KT + u) * HG + h
                if u == 0 and h == 0:
                    pe.wait_ge(maxT_copied, n * HG + HG)
                    if j == 0:
                        pe.wait_ge(exp_done, c)
                if not (u == 0 and h == 0 and j == 0):
                    pe.wait_ge(exp_done, c - 1)
                nc.tensor.matmul(s_ps[:, h % 2], k_sb[0:XROWS, j // GPB, h, u * P:(u + 1) * P],
                                 q_sb[0:XROWS, j % QR, h], start=True, stop=True).then_inc(s_ready, 1)

            def values(n, j, u, it):
                pe.wait_ge(exp_done, (n * KT + u + 1) * HG)
                if u == 0:
                    pe.wait_ge(o_copied, n)
                    if j % GPB == 0:
                        pe.wait_ge(v_loaded[j // GPB], 16 * (it + 1))
                for h in range(HG):
                    last = nc.tensor.matmul(o_ps[32 * h:32 * h + AUG], v_sb[:, j // GPB, u, h * AUG:(h + 1) * AUG],
                                            probs[:, u % 2, h], start=(u == 0), stop=(u == KT - 1))
                last.then_inc(pv_done, 1)

            def turn_result(n):
                pe.wait_ge(o_copied, n + 1)
                for t in range(TPG):
                    last = nc.tensor.transpose(turn_ps[:, t], o_sb[:, t * P:(t + 1) * P], m.ident[:])
                last.then_inc(turned, 1)

            pe.wait_ge(rows_set, 1)
            pe.wait_ge(o_zeroed, 1)
            for _ in items(0, 0, range(MAXI), 0):
                pass
            for _ in items(1, 1, range(2 * LEAD), 0):
                pass
            for r in range(2):
                turn_maxima(pe, 0, r)
            with pe.Fori(0, NIT) as it:
                for j in range(NB):
                    n = it * NB + j
                    for u in range(KT):
                        k = 2 * (u + LEAD)
                        ahead = 1 + k // MAXI
                        share = items(n + ahead, (j + ahead) % NB, (k % MAXI, k % MAXI + 1),
                                      it + (j + ahead) // NB)
                        if u == 2 and j > 0:
                            turn_result(n - 1)
                        scores(n, j, u, 0)
                        scores(n, j, u, 1)
                        if u > 0:
                            values(n, j, u - 1, it)
                        elif j > 0:
                            values(n - 1, j - 1, KT - 1, it)
                        scores(n, j, u, 2)
                        scores(n, j, u, 3)
                        if u in TURN_AT:
                            turn_maxima(pe, n + 1, TURN_AT.index(u))
                        next(share)
                        next(share)
                        next(share)
                        next(share)
                values(n, NB - 1, KT - 1, it)
                pe.wait_ge(maxT_copied, (n + 2) * HG)
                turn_result(n)

        @block.scalar
        def _(act):
            def exps(n, u, h):
                c = (n * KT + u) * HG + h
                act.wait_ge(s_ready, c + 1)
                nc.scalar.activation(probs[:, u % 2, h], s_ps[:, h % 2], ACT.Exp, scale=float(HD) ** -0.5).then_inc(exp_done, 1)

            def copy_result(n):
                act.wait_ge(pv_done, (n + 1) * KT)
                act.wait_ge(turned, n)
                nc.scalar.activation(o_sb[:], o_ps[:], ACT.Copy).then_inc(o_copied, 1)

            for h in range(HG):
                copy_maxima(act, 0, 0, h)
            with act.Fori(0, NIT) as it:
                for j in range(NB):
                    n = it * NB + j
                    for u in range(KT):
                        for h in range(HG):
                            if h == 0:
                                if j > 0 or u > 1:
                                    act.wait_ge(pv_done, n * KT + u - 1)
                                elif u == 1:
                                    act.wait_ge(pv_done, n * KT)
                            if u == 0 and h == 3 and j > 0:
                                copy_result(n - 1)
                            exps(n, u, h)
                        if u in COPY_AT:
                            copy_maxima(act, n + 1, (j + 1) % NB, COPY_AT.index(u))
                copy_result(n)

        @block.vector
        def _(dve):
            heads = turn_ps[:].rearrange("p t (h c) -> p t h c", h=HG)

            def divide(n, it, j, s):
                if s == 0:
                    dve.wait_ge(turned, n + 1)
                    nc.vector.reciprocal(inv[:], heads[:, :, :, HD]).then_inc(inv_ready, 1)
                else:
                    dve.wait_ge(inv_ready, n + 1)
                    dst = att[:, ds(it, 1), j // GPB, (j % GPB) * TPG:(j % GPB + 1) * TPG].rearrange("p a t (h c) -> p (a t) h c", h=HG)
                    nc.vector.tensor_tensor(dst, heads[:, :, :, 0:HD], inv[:].unsqueeze(3).broadcast_to([P, TPG, HG, HD]),
                                            ALU.mult).then_inc(att_done, 1)

            nc.vector.memset(o_ps[:], 0.0).then_inc(o_zeroed, 1)
            for k in range(MAXI):
                max_take(dve, 0, 0, k)
            for k in range(2 * LEAD):
                max_take(dve, 1, 1, k)
                row_maxima(dve, 0, 0, k)
            with dve.Fori(0, NIT) as it:
                for j in range(NB):
                    n = it * NB + j
                    for u in range(KT):
                        for i in range(2):
                            k = 2 * (u + LEAD) + i
                            ahead = 1 + k // MAXI
                            max_take(dve, n + ahead, (j + ahead) % NB, k % MAXI)
                            if KT - LEAD <= u < KT - LEAD + 3:
                                row_maxima(dve, n + 1, (j + 1) % NB, 2 * (u - (KT - LEAD)) + i)
                            if u == 3 and j > 0:
                                divide(n - 1, it, j - 1, i)
                for i in range(2):
                    divide(n, it, NB - 1, i)
            dve.wait_ge(att_done, NIT * NB)


def wo_buffers(ctx, nc, tag, aT_ps=None, y_ps=None):
    sb, pb, sem = allocators(ctx, nc, tag)
    return named(
        a=sb("wo_a", [P, TPG, D]), aT=sb("wo_aT", [P, KH, G]), y=sb("wo_y", [P, TPG, D]), w=sb("wo_w", [P, KH, D]),
        aT_ps=pb("wo_aT_ps", [P, KH, G]) if aT_ps is None else aT_ps,
        y_ps=pb("wo_y_ps", [P, TPG, D]) if y_ps is None else y_ps,
        w_loaded=sem("wo_w_loaded"), a_ready=sem("wo_a_ready"), a_turned=sem("wo_a_turned"),
        aT_copied=sem("wo_aT_copied"), y_ready=sem("wo_y_ready"), y_scaled=sem("wo_y_scaled"), x_added=sem("wo_x_added"))


def wo_tensor(nc, pe, m, wo, n, a_count):
    pe.wait_ge(wo.a_ready, a_count)
    pe.wait_ge(wo.aT_copied, n * KH)
    for t in range(TPG):
        for half in range(KH):
            last = nc.tensor.transpose(wo.aT_ps[:, half, t * P:(t + 1) * P], wo.a[:, t, half * P:(half + 1) * P], m.ident[:])
    last.then_inc(wo.a_turned, 1)
    pe.wait_ge(wo.aT_copied, n * KH + KH)
    pe.wait_ge(wo.y_scaled, n * 2)
    for t in range(TPG):
        for kh in range(KH):
            last = nc.tensor.matmul(wo.y_ps[:, t], wo.aT[:, kh, t * P:(t + 1) * P], wo.w[:, kh],
                                    start=(kh == 0), stop=(kh == KH - 1))
        if t % 2:
            last.then_inc(wo.y_ready, 1)


def wo_scalar(nc, act, wo, n):
    act.wait_ge(wo.a_turned, n + 1)
    act.wait_ge(wo.y_ready, n * 2)
    for half in range(KH):
        nc.scalar.activation(wo.aT[:, half], wo.aT_ps[:, half], ACT.Copy).then_inc(wo.aT_copied, 1)


def wo_vector(nc, dve, m, wo, n, b, layer):
    for pair in range(2):
        dve.wait_ge(wo.y_ready, n * 2 + pair + 1)
        gate = m.gates[:, layer, 0, ds(b, 1)].broadcast_to([P, 2, D])
        nc.vector.tensor_tensor(wo.y[:, 2 * pair:2 * pair + 2], wo.y_ps[:, 2 * pair:2 * pair + 2], gate, ALU.mult).then_inc(wo.y_scaled, 1)
    for pair in range(2):
        dve.wait_ge(wo.y_scaled, n * 2 + pair + 1)
        xs = m.x[:, ds(n * TPG + 2 * pair, 2)]
        nc.vector.tensor_tensor(xs, xs, wo.y[:, 2 * pair:2 * pair + 2], ALU.add).then_inc(wo.x_added, 1)
    dve.wait_ge(wo.x_added, n * 2 + 2)


ROUTE_STEPS = 2 + 1 + 1 + 1 + TPG + TPG + 1 + 2


def route_buffers(ctx, nc, tag, E):
    sb, pb, sem = allocators(ctx, nc, tag)
    return named(
        E=E, logits=sb("rt_logits", [P, TPG, E]), mx=sb("rt_mx", [P, TPG]), e=sb("rt_e", [P, TPG, E]),
        tot=sb("rt_tot", [P, TPG]), p=sb("rt_p", [P, TPG, E]), top=sb("rt_top", [P, TPG, 8]),
        idx=sb("rt_idx", [P, TPG, 8], U32), idx_f=sb("rt_idx_f", [P, TPG, 2]), hot=sb("rt_hot", [P, 2, TPG, E]),
        logits_ready=sem("rt_logits_ready"), shifted=sem("rt_shifted"), exp_ready=sem("rt_exp_ready"), step=sem("rt_step"))


def route_scalar(nc, act, rt, n):
    act.wait_ge(rt.shifted, n + 1)
    nc.scalar.activation(rt.e[:], rt.logits[:], ACT.Exp).then_inc(rt.exp_ready, 1)


def route_vector(nc, dve, m, rt, n, logits_ps, bias=None):
    E = rt.E
    done = [0]

    def step(ins):
        ins.then_inc(rt.step, 1)
        done[0] += 1

    def steps_done():
        dve.wait_ge(rt.step, n * ROUTE_STEPS + done[0])

    wide = lambda a: a.unsqueeze(2).broadcast_to([P, TPG, E])
    dve.wait_ge(rt.logits_ready, n + 1)
    if bias is None:
        step(nc.vector.tensor_copy(rt.p[:], logits_ps))
    else:
        step(nc.vector.tensor_tensor(rt.p[:], logits_ps, bias.unsqueeze(1).broadcast_to([P, TPG, E]), ALU.add))
    steps_done()
    step(nc.vector.reduce_max(rt.mx[:], rt.p[:], AX.X))
    steps_done()
    nc.vector.tensor_tensor(rt.logits[:], rt.p[:], wide(rt.mx[:]), ALU.subtract).then_inc(rt.shifted, 1)
    dve.wait_ge(rt.exp_ready, n + 1)
    step(nc.vector.reduce_sum(rt.tot[:], rt.e[:], AX.X))
    steps_done()
    step(nc.vector.reciprocal(rt.tot[:], rt.tot[:]))
    steps_done()
    step(nc.vector.tensor_tensor(rt.p[:], rt.e[:], wide(rt.tot[:]), ALU.mult))
    steps_done()
    settle(dve, m)
    for t in range(TPG):
        step(nc.vector.max(rt.top[:, t], rt.p[:, t]))
    steps_done()
    settle(dve, m)
    for t in range(TPG):
        step(nc.vector.max_index(rt.idx[:, t], rt.top[:, t], rt.p[:, t]))
    steps_done()
    step(nc.vector.tensor_copy(rt.idx_f[:], rt.idx[:, :, 0:2]))
    steps_done()
    for k in range(2):
        step(nc.vector.tensor_tensor(rt.hot[:, k], wide(rt.idx_f[:, :, k]),
                                     m.iota[:, 0:E].unsqueeze(1).broadcast_to([P, TPG, E]), ALU.is_equal))
    steps_done()
    assert done[0] == ROUTE_STEPS


def finish_attention0_and_route(nc, m, io):
    with ExitStack() as ctx:
        sb, pb, sem = allocators(ctx, nc, "post0")
        ln, wo, rt = ln_buffers(ctx, nc, "post0"), wo_buffers(ctx, nc, "post0"), route_buffers(ctx, nc, "post0", E0)
        w_router = sb("w_router", [P, KH, E0])
        logits_ps = pb("logits_ps", [P, TPG, E0])
        loaded, z_kept, routed = sem("loaded"), sem("z_kept"), sem("routed")
        att = m.att
        block = ctx.enter_context(nc.Block())

        @block.sync
        def _(sync):
            sync.dma_start(wo.w[:], io.l0_wo).then_inc(wo.w_loaded, 16)
            sync.dma_start(w_router[:], io.w_router).then_inc(loaded, 16)

        @block.tensor
        def _(pe):
            pe.wait_ge(wo.w_loaded, 16)
            pe.wait_ge(loaded, 16)
            with pe.Fori(0, B) as b:
                with pe.Fori(0, GPB) as q:
                    n = group_of(b, q)
                    wo_tensor(nc, pe, m, wo, n, n + 1)
                    ln_tensor(nc, pe, m, ln, n)
                    pe.wait_ge(ln.h_ready, n * KH + KH)
                    pe.wait_ge(rt.step, n * ROUTE_STEPS)
                    for t in range(TPG):
                        for kh in range(KH):
                            last = nc.tensor.matmul(logits_ps[:, t], ln.hT[:, kh, t * P:(t + 1) * P], w_router[:, kh],
                                                    start=(kh == 0), stop=(kh == KH - 1))
                    last.then_inc(rt.logits_ready, 1)

        @block.scalar
        def _(act):
            with act.Fori(0, B) as b:
                with act.Fori(0, GPB) as q:
                    n = group_of(b, q)
                    act.wait_ge(wo.a_turned, n)
                    src = att[:, ds(b, 1), :, ds(q * TPG, TPG)].rearrange("p a g t c -> p (a g) t c")
                    nc.scalar.activation(wo.a[:].rearrange("p t (g c) -> p g t c", g=NHG), src, ACT.Copy).then_inc(wo.a_ready, 1)
                    wo_scalar(nc, act, wo, n)
                    ln_scalar(nc, act, m, ln, n, b, 0, 1, lambda: act.wait_ge(rt.logits_ready, n))
                    dst = m.z_all[:, ds(n * TPG, TPG)]
                    act.wait_ge(ln.z_ready, n * TPG + TPG)
                    nc.scalar.activation(dst, ln.z[:], ACT.Copy).then_inc(z_kept, 1)
                    route_scalar(nc, act, rt, n)

        @block.vector
        def _(dve):
            with dve.Fori(0, B) as b:
                with dve.Fori(0, GPB) as q:
                    n = group_of(b, q)
                    wo_vector(nc, dve, m, wo, n, b, 0)
                    ln_vector(nc, dve, m, ln, n, lambda: dve.wait_ge(z_kept, n), None)
                    route_vector(nc, dve, m, rt, n, logits_ps[:])
                    at = (ds(b, 1), slice(None), ds(q * TPG, TPG))
                    one = lambda a: a.rearrange("p k t -> p k t").unsqueeze(1)
                    nc.vector.tensor_copy(m.top_p[:, ds(b, 1), :, ds(q * TPG, TPG)].rearrange("p a k t -> p (a k) t"),
                                          rt.top[:, :, 0:2].rearrange("p t k -> p k t")).then_inc(routed, 1)
                    nc.vector.tensor_copy(m.top_e[:, ds(b, 1), :, ds(q * TPG, TPG)].rearrange("p a k t -> p (a k) t"),
                                          rt.idx_f[:].rearrange("p t k -> p k t")).then_inc(routed, 1)
                    nc.vector.tensor_copy(m.chosen[:, ds(b, 1), :, ds(q * TPG, TPG)].rearrange("p a k t e -> p (a k) (t e)"),
                                          rt.hot[:].rearrange("p k t e -> p k (t e)")).then_inc(routed, 1)
                    dve.wait_ge(routed, n * 3 + 3)


def layer0_experts(nc, m, io):
    with ExitStack() as ctx:
        sb, pb, sem = allocators(ctx, nc, "slots")
        put_at = sb("put_at", [P, B, 2, TPB], I32)
        get_at = sb("get_at", [P, B, 2, TPB], I32)
        dispatch(nc, m, io, put_at, get_at)
        run_experts(nc, m, io)
        collect(nc, m, io, get_at)


def dispatch(nc, m, io, put_at, get_at):
    with ExitStack() as ctx:
        sb, pb, sem = allocators(ctx, nc, "disp")
        S = 2 * TPB
        ones = sb("ones", [P, P], BF16)
        before = [sb(f"before{i}", [P, B, S, E0]) for i in range(2)]
        place = sb("place", [P, B, S, E0])
        pos = sb("pos", [P, B, S])
        base = sb("base", [P, B, S])
        over = sb("over", [P, B, S])
        spot = sb("spot", [P, 2, B, S])
        upto_ps = pb("upto_ps", [P, B, S, E0])
        tile_ps = pb("tile_ps", [P, B, S, E0])
        ones_set, counted, step, put_ready, rows_put = sem("ones_set"), sem("counted"), sem("step"), sem("put_ready"), sem("rows_put")
        block = ctx.enter_context(nc.Block())

        @block.tensor
        def _(pe):
            pe.wait_ge(ones_set, 1)
            for b in range(B):
                hot = m.chosen[:, b].rearrange("p k t e -> p (k t e)")
                nc.tensor.matmul(upto_ps[:, b].rearrange("p s e -> p (s e)"), m.triu_b[:], hot, start=True, stop=True)
                nc.tensor.matmul(tile_ps[:, b].rearrange("p s e -> p (s e)"), ones[:], hot, start=True, stop=True).then_inc(counted, 1)

        @block.vector
        def _(dve):
            n = [0]

            def step_done(*instructions):
                for ins in instructions:
                    ins.then_inc(step, 1)
                    n[0] += 1
                dve.wait_ge(step, n[0])

            nc.vector.memset(ones[:], 1.0).then_inc(ones_set, 1)
            dve.wait_ge(counted, B)
            step_done(nc.vector.memset(before[0][:, :, 0], 0.0),
                      nc.vector.tensor_copy(before[0][:, :, 1:S], tile_ps[:, :, 0:S - 1]))
            src, d = 0, 1
            while d < S:
                a, c = before[src], before[1 - src]
                step_done(nc.vector.tensor_tensor(c[:, :, d:S], a[:, :, d:S], a[:, :, 0:S - d], ALU.add),
                          nc.vector.tensor_copy(c[:, :, 0:d], a[:, :, 0:d]))
                src, d = 1 - src, 2 * d
            hot = m.chosen[:].rearrange("p b k t e -> p b (k t) e")
            step_done(nc.vector.tensor_tensor(place[:], upto_ps[:], before[src][:], ALU.add))
            step_done(nc.vector.tensor_tensor(place[:], place[:], hot, ALU.mult))
            step_done(nc.vector.reduce_sum(pos[:], place[:], AX.X))
            e = m.top_e[:].rearrange("p b k t -> p b (k t)")
            step_done(*[nc.vector.tensor_scalar(base[:, b], e[:, b], float(B * CAP), float(b * CAP - 1), ALU.mult, ALU.add)
                        for b in range(B)],
                      nc.vector.tensor_scalar(over[:], pos[:], float(CAP), float(2 * SLOTS), ALU.is_gt, ALU.mult))
            step_done(nc.vector.tensor_tensor(over[:], over[:], base[:], ALU.add),
                      nc.vector.tensor_scalar(spot[:, 1], pos[:], float(CAP), None, ALU.min))
            step_done(nc.vector.tensor_tensor(spot[:, 0], over[:], pos[:], ALU.add),
                      nc.vector.tensor_tensor(spot[:, 1], spot[:, 1], base[:], ALU.add))
            nc.vector.tensor_copy(put_at[:].rearrange("p b k t -> p b (k t)"), spot[:, 0]).then_inc(put_ready, 1)
            nc.vector.tensor_copy(get_at[:].rearrange("p b k t -> p b (k t)"), spot[:, 1]).then_inc(put_ready, 1)
            dve.wait_ge(put_ready, 2)

        @block.gpsimd
        def _(pool):
            pool.wait_ge(put_ready, 2)
            for b in range(B):
                for k in range(2):
                    for t in range(TPB):
                        nc.gpsimd.indirect_dma_start(
                            out=io.slot_rows, out_offset=bass.IndirectOffsetOnAxis(ap=put_at[:, b, k, t:t + 1], axis=0),
                            in_=m.z_all[:, b * TPB + t], in_offset=None,
                            bounds_check=SLOTS - 1, oob_is_err=False).then_inc(rows_put, 16)
            pool.wait_ge(rows_put, 16 * B * 2 * TPB)


def run_experts(nc, m, io):
    with ExitStack() as ctx:
        sb, pb, sem = allocators(ctx, nc, "moe")
        ET = B * CAP // P
        NSL = B * CAP
        rows = sb("rows", [P, 2, ET, D])
        w_gf = sb("w_gf", [P, 2, KH, 2 * HID])
        w_pr = sb("w_pr", [P, 2, D])
        hT = sb("hT", [P, KH, NSL])
        act_gate = sb("act_gate", [P, NSL])
        hid = sb("hid", [P, NSL])
        y = sb("y", [P, 2, ET, D])
        rT_ps, gf_ps, y_ps = pb("rT_ps", [P, KH, NSL]), pb("gf_ps", [P, 2, NSL]), pb("y_ps", [P, ET, D])
        loaded = [sem(f"loaded{r}") for r in range(2)]
        stored = [sem(f"stored{r}") for r in range(2)]
        turned, h_ready, gf_ready, silu_ready, hid_ready = sem("turned"), sem("h_ready"), sem("gf_ready"), sem("silu_ready"), sem("hid_ready")
        y_ready, y_scaled = sem("y_ready"), sem("y_scaled")
        block = ctx.enter_context(nc.Block())
        tiles = lambda dram: dram.rearrange("(e t p) d -> e p t d", e=E0, p=P)

        @block.sync
        def _(sync):
            def load(e, r):
                sync.dma_start(rows[:, r], tiles(io.slot_rows)[ds(e, 1)].rearrange("a p t d -> (a p) t d")).then_inc(loaded[r], 16)
                sync.dma_start(w_gf[:, r], io.w_gate_fc[ds(e, 1)].rearrange("a p k n -> (a p) k n")).then_inc(loaded[r], 16)
                sync.dma_start(w_pr[:, r], io.w_proj[ds(e, 1)].rearrange("a p n -> (a p) n")).then_inc(loaded[r], 16)

            for r in range(2):
                load(r, r)
            with sync.Fori(0, E0 // 2 - 1) as i:
                for r in range(2):
                    sync.wait_ge(y_ready, (i * 2 + r + 1) * 2)
                    load(i * 2 + r + 2, r)

        @block.gpsimd
        def _(pool):
            with pool.Fori(0, E0 // 2) as i:
                for r in range(2):
                    e = i * 2 + r
                    pool.wait_ge(y_scaled, e * 2 + 2)
                    pool.dma_start(tiles(io.slot_out)[ds(e, 1)].rearrange("a p t d -> (a p) t d"), y[:, r]).then_inc(stored[r], 16)
            for r in range(2):
                pool.wait_ge(stored[r], 16 * (E0 // 2))

        @block.tensor
        def _(pe):
            with pe.Fori(0, E0 // 2) as i:
                for r in range(2):
                    e = i * 2 + r
                    pe.wait_ge(loaded[r], 48 * (i + 1))
                    pe.wait_ge(h_ready, e * 2 * KH)
                    for t in range(ET):
                        for half in range(KH):
                            last = nc.tensor.transpose(rT_ps[:, half, t * P:(t + 1) * P], rows[:, r, t, half * P:(half + 1) * P], m.ident[:])
                    last.then_inc(turned, 1)
                    pe.wait_ge(h_ready, (e + 1) * 2 * KH)
                    pe.wait_ge(hid_ready, e)
                    for v in range(2):
                        for kh in range(KH):
                            last = nc.tensor.matmul(gf_ps[:, v], w_gf[:, r, kh, v * HID:(v + 1) * HID], hT[:, kh],
                                                    start=(kh == 0), stop=(kh == KH - 1))
                        last.then_inc(gf_ready, 1)
                    pe.wait_ge(hid_ready, e + 1)
                    pe.wait_ge(y_scaled, e * 2)
                    for t in range(ET):
                        last = nc.tensor.matmul(y_ps[:, t], hid[:, t * P:(t + 1) * P], w_pr[:, r], start=True, stop=True)
                        if t % 2:
                            last.then_inc(y_ready, 1)

        @block.scalar
        def _(act):
            with act.Fori(0, E0 // 2) as i:
                for r in range(2):
                    e = i * 2 + r
                    act.wait_ge(turned, e + 1)
                    act.wait_ge(gf_ready, e * 2)
                    for half in range(KH):
                        for b in range(B):
                            cols = slice(b * CAP, (b + 1) * CAP)
                            nc.scalar.activation(hT[:, half, cols], rT_ps[:, half, cols], ACT.Identity,
                                                 bias=m.modv[:, 0, 2, half, b:b + 1],
                                                 scale=m.modv[:, 0, 3, half, b:b + 1]).then_inc(h_ready, 1)
                    act.wait_ge(gf_ready, e * 2 + 1)
                    act.wait_ge(hid_ready, e)
                    nc.scalar.activation(act_gate[:], gf_ps[:, 0], ACT.Silu).then_inc(silu_ready, 1)

        @block.vector
        def _(dve):
            with dve.Fori(0, E0 // 2) as i:
                for r in range(2):
                    e = i * 2 + r
                    dve.wait_ge(silu_ready, e + 1)
                    dve.wait_ge(gf_ready, e * 2 + 2)
                    dve.wait_ge(y_ready, e * 2)
                    nc.vector.tensor_tensor(hid[:], act_gate[:], gf_ps[:, 1], ALU.mult).then_inc(hid_ready, 1)
                    dve.wait_ge(stored[r], i * 16)
                    for b in range(B):
                        dve.wait_ge(y_ready, e * 2 + b + 1)
                        gate = m.gates[:, 0, 1, b].unsqueeze(1).broadcast_to([P, 2, D])
                        nc.vector.tensor_tensor(y[:, r, 2 * b:2 * b + 2], y_ps[:, 2 * b:2 * b + 2], gate, ALU.mult).then_inc(y_scaled, 1)


def collect(nc, m, io, get_at):
    with ExitStack() as ctx:
        sb, pb, sem = allocators(ctx, nc, "coll")
        RING = 8
        got = sb("got", [P, RING, 2, D])
        rows_in = [sem(f"rows_in{r}") for r in range(RING)]
        added = sem("added")
        block = ctx.enter_context(nc.Block())

        @block.gpsimd
        def _(pool):
            for t in range(NT):
                if t >= RING:
                    pool.wait_ge(added, 2 * (t - RING + 1))
                for k in range(2):
                    nc.gpsimd.indirect_dma_start(
                        out=got[:, t % RING, k], out_offset=None, in_=io.slot_out,
                        in_offset=bass.IndirectOffsetOnAxis(ap=get_at[:, t // TPB, k, t % TPB:t % TPB + 1], axis=0),
                        bounds_check=SLOTS - 1, oob_is_err=False).then_inc(rows_in[t % RING], 16)

        @block.vector
        def _(dve):
            for t in range(NT):
                dve.wait_ge(rows_in[t % RING], 32 * (t // RING + 1))
                for k in range(2):
                    if k:
                        dve.wait_ge(added, 2 * t + 1)
                    nc.vector.scalar_tensor_tensor(m.x[:, t], got[:, t % RING, k], m.top_p[:, t // TPB, k, t % TPB:t % TPB + 1],
                                                   m.x[:, t], ALU.mult, ALU.add).then_inc(added, 1)
            dve.wait_ge(added, 2 * NT)


def linear_attention(nc, m, io):
    with ExitStack() as ctx:
        sb, pb, sem = allocators(ctx, nc, "lin")
        ln = ln_buffers(ctx, nc, "lin")
        HV = NHH * AUG
        qk_ps = pb("qk_ps", [P, 4, G])
        kv_ps = pb("kv_ps", [P, 2 * D])
        o_ps = pb("o_ps", [P, NH * AUG])
        st_ps = ln.zT[:, 0, 0:NH * AUG]
        wo = wo_buffers(ctx, nc, "lin", ln.zT, qk_ps[:, 0:2].rearrange("p a n -> p (a n)").rearrange("p (t d) -> p t d", d=D))
        w_qk, w_kv = sb("w_qk", [P, KH, 2 * D]), sb("w_kv", [P, KH, 2 * D])
        head_of = sb("head_of", [P, NHH])
        qkT = sb("qkT", [P, 4, G])
        q_wide = sb("q_wide", [P, 2, NHH, P])
        masked = sb("masked", [P, 2, NHH, P])
        k_tok = sb("k_tok", [P, D])
        va = sb("va", [P, NH * AUG])
        kv_new = sb("kv_new", [P, 2, HV])
        kv_state = sb("kv_state", [P, 2, HV])
        den = sb("den", [P, NH])
        loaded, ones_set = sem("loaded"), sem("ones_set")
        qk_ready, qk_copied, wide_ready = sem("qk_ready"), sem("qk_copied"), sem("wide_ready")
        kv_ready, k_copied, v_copied = sem("kv_ready"), sem("k_copied"), sem("v_copied")
        s_ready, masked_ready, o_ready = sem("s_ready"), sem("masked_ready"), sem("o_ready")
        st_ready, st_masked, st_added, den_step = sem("st_ready"), sem("st_masked"), sem("st_added"), sem("den_step")
        block = ctx.enter_context(nc.Block())
        TB1 = TPB + 1

        @block.sync
        def _(sync):
            sync.dma_start(w_qk[:], io.l1_wqk).then_inc(loaded, 16)
            sync.dma_start(w_kv[:], io.l1_wkv).then_inc(loaded, 16)
            sync.dma_start(head_of[:], io.head_of).then_inc(loaded, 16)
            sync.dma_start(wo.w[:], io.l1_wo).then_inc(loaded, 16)

        @block.gpsimd
        def _(pool):
            nc.gpsimd.memset(va[:].rearrange("p (h c) -> p h c", c=AUG)[:, :, HD:AUG], 1.0).then_inc(ones_set, 1)

        @block.tensor
        def _(pe):
            pe.wait_ge(loaded, 64)
            pe.wait_ge(ones_set, 1)
            with pe.Fori(0, B) as b:
                with pe.Fori(0, GPB) as q:
                    n = group_of(b, q)
                    pe.wait_ge(wo.aT_copied, n * KH)
                    ln_tensor(nc, pe, m, ln, n)
                    pe.wait_ge(ln.h_ready, n * KH + KH)
                    pe.wait_ge(wo.y_scaled, n * 2)
                    for a in range(4):
                        for kh in range(KH):
                            last = nc.tensor.matmul(qk_ps[:, a], w_qk[:, kh, a * P:(a + 1) * P], ln.hT[:, kh],
                                                    start=(kh == 0), stop=(kh == KH - 1))
                        last.then_inc(qk_ready, 1)
                    for t in range(TPG):
                        c = n * TPG + t
                        tok = slice(t * P, (t + 1) * P)
                        pe.wait_ge(k_copied, c)
                        pe.wait_ge(v_copied, c)
                        for kh in range(KH):
                            last = nc.tensor.matmul(kv_ps[:], ln.hT[:, kh, tok], w_kv[:, kh],
                                                    start=(kh == 0), stop=(kh == KH - 1))
                        last.then_inc(kv_ready, 1)
                        pe.wait_ge(qk_copied, n * 4 + 4)
                        pe.wait_ge(masked_ready, c * 2)
                        for half in range(2):
                            pe.wait_ge(wide_ready, c * 2 + half + 1)
                            for g in range(2):
                                last = nc.tensor.matmul(qk_ps[:, 2 * half + g], qkT[:, 2 + half, tok],
                                                        q_wide[:, half, g * HG:(g + 1) * HG].rearrange("p h n -> p (h n)"),
                                                        start=True, stop=True)
                            last.then_inc(s_ready, 1)
                        pe.wait_ge(wo.a_ready, c)
                        pe.wait_ge(st_added, b * TB1 + q * TPG + t + 1)
                        pe.wait_ge(v_copied, c + 1)
                        for half in range(2):
                            nc.tensor.matmul(o_ps[:, half * HV:(half + 1) * HV], qkT[:, half, tok], kv_state[:, half],
                                             start=True, stop=False, skip_group_check=True)
                            pe.wait_ge(masked_ready, c * 2 + half + 1)
                            for h in range(NHH):
                                cols = slice((half * NHH + h) * AUG, (half * NHH + h + 1) * AUG)
                                last = nc.tensor.matmul(o_ps[:, cols], masked[:, half, h], va[:, cols],
                                                        start=False, stop=(h == NHH - 1), skip_group_check=True)
                        last.then_inc(o_ready, 1)
                        pe.wait_ge(k_copied, c + 1)
                        for half in range(2):
                            last = nc.tensor.matmul(st_ps[:, half * HV:(half + 1) * HV], k_tok[:, half * HALF:(half + 1) * HALF],
                                                    va[:, half * HV:(half + 1) * HV], start=True, stop=True)
                        last.then_inc(st_ready, 1)
                    pe.wait_ge(st_added, b * TB1 + q * TPG + TPG + 1)
                    pe.wait_ge(masked_ready, n * TPG * 2 + TPG * 2)
                    wo_tensor(nc, pe, m, wo, n, n * TPG + TPG)

        @block.scalar
        def _(act):
            act.wait_ge(ones_set, 1)
            with act.Fori(0, B) as b:
                with act.Fori(0, GPB) as q:
                    n = group_of(b, q)
                    ln_scalar(nc, act, m, ln, n, b, 1, 0, lambda: act.wait_ge(kv_ready, n * TPG))
                    for t in range(TPG):
                        c = n * TPG + t
                        act.wait_ge(kv_ready, c + 1)
                        act.wait_ge(st_ready, c)
                        nc.scalar.activation(va[:].rearrange("p (h c) -> p h c", c=AUG)[:, :, 0:HD],
                                             kv_ps[:, D:2 * D].rearrange("p (h c) -> p h c", c=HD), ACT.Copy).then_inc(v_copied, 1)
                    wo_scalar(nc, act, wo, n)

        @block.vector
        def _(dve):
            dve.wait_ge(loaded, 64)
            with dve.Fori(0, B) as b:
                dve.wait_ge(o_ready, b * TPB)
                nc.vector.memset(kv_state[:], 0.0).then_inc(st_added, 1)
                with dve.Fori(0, GPB) as q:
                    n = group_of(b, q)
                    ln_vector(nc, dve, m, ln, n, lambda: None, None)
                    dve.wait_ge(o_ready, n * TPG)
                    for a in range(4):
                        dve.wait_ge(qk_ready, n * 4 + a + 1)
                        nc.vector.tensor_scalar(qkT[:, a], qk_ps[:, a], 0.0, EPS_LIN, ALU.max, ALU.add).then_inc(qk_copied, 1)
                    dve.wait_ge(qk_copied, n * 4 + 4)
                    for t in range(TPG):
                        c = n * TPG + t
                        dve.wait_ge(s_ready, c * 2)
                        for half in range(2):
                            nc.vector.tensor_tensor(q_wide[:, half],
                                                    qkT[:, half, t * P:(t + 1) * P].unsqueeze(1).broadcast_to([P, NHH, P]),
                                                    head_of[:].unsqueeze(2).broadcast_to([P, NHH, P]), ALU.mult).then_inc(wide_ready, 1)
                        dve.wait_ge(v_copied, c + 1)
                        dve.wait_ge(st_ready, c)
                        nc.vector.tensor_scalar(k_tok[:], kv_ps[:, 0:D], 0.0, EPS_LIN, ALU.max, ALU.add).then_inc(k_copied, 1)
                        for half in range(2):
                            dve.wait_ge(s_ready, c * 2 + half + 1)
                            nc.vector.tensor_tensor(masked[:, half],
                                                    qk_ps[:, 2 * half:2 * half + 2].rearrange("p g (h n) -> p (g h) n", n=P),
                                                    m.triu[:].unsqueeze(1).broadcast_to([P, NHH, P]), ALU.mult).then_inc(masked_ready, 1)
                        dve.wait_ge(st_ready, c + 1)
                        nc.vector.tensor_tensor(kv_new[:].rearrange("p a (h c) -> p a h c", c=AUG),
                                                st_ps.rearrange("p (a h c) -> p a h c", a=2, c=AUG),
                                                head_of[:].unsqueeze(1).unsqueeze(3).broadcast_to([P, 2, NHH, AUG]),
                                                ALU.mult).then_inc(st_masked, 1)
                        dve.wait_ge(o_ready, c + 1)
                        heads = o_ps[:].rearrange("p (h c) -> p h c", c=AUG)
                        nc.vector.tensor_scalar(den[:], heads[:, :, HD], EPS_LIN, None, ALU.add).then_inc(den_step, 1)
                        dve.wait_ge(st_masked, c + 1)
                        nc.vector.tensor_tensor(kv_state[:], kv_state[:], kv_new[:], ALU.add).then_inc(st_added, 1)
                        dve.wait_ge(den_step, c * 2 + 1)
                        nc.vector.reciprocal(den[:], den[:]).then_inc(den_step, 1)
                        dve.wait_ge(den_step, c * 2 + 2)
                        if t == 0:
                            dve.wait_ge(wo.a_turned, n)
                        nc.vector.tensor_tensor(wo.a[:, t].rearrange("p (h c) -> p h c", c=HD), heads[:, :, 0:HD],
                                                den[:].unsqueeze(2).broadcast_to([P, NH, HD]), ALU.mult).then_inc(wo.a_ready, 1)
                    wo_vector(nc, dve, m, wo, n, b, 1)


def project_layer1_ffn(nc, m, io):
    with ExitStack() as ctx:
        sb, pb, sem = allocators(ctx, nc, "ffn1")
        ln, sp, rt = ln_buffers(ctx, nc, "ffn1"), split_buffers(ctx, nc, "ffn1"), route_buffers(ctx, nc, "ffn1", E1)
        w_qkv, b_qk, b_v = sb("w_qkv", [P, KH, 3 * D]), sb("b_qk", [P, 4]), sb("b_v", [P, D])
        w_gate, b_gate = sb("w_gate", [P, KH, E1]), sb("b_gate", [P, E1])
        w_exp, b_exp = sb("w_exp", [P, KH, E1 * D]), sb("b_exp", [E1, D])
        va = sb("va", [P, TPG, NH * AUG])
        shares = sb("shares", [P, 2, TPG, E1])
        comb = sb("comb", [P, TPG, E1])
        combT = sb("combT", [E1, TPG, P])
        acc = sb("acc", [P, TPG, D])
        acc_g = sb("acc_g", [P, TPG, D])
        qk_ps = pb("qk_ps", [P, 4, G])
        v_ps = pb("v_ps", [P, TPG, D])
        logits_ps = ln.zT[:, 0, 0:TPG * E1].rearrange("p (t e) -> p t e", e=E1)
        combT_ps = ln.zT[0:E1, 1].rearrange("p (t n) -> p t n", n=P)
        loaded, ones_set = sem("loaded"), sem("ones_set")
        qk_ready, v_ready, v_copied, v_stored = sem("qk_ready"), sem("v_ready"), sem("v_copied"), sem("v_stored")
        share_ready, comb_ready, combT_ready, combT_copied = sem("share_ready"), sem("comb_ready"), sem("combT_ready"), sem("combT_copied")
        bias_ready, ex_ready, acc_step, gated, x_added = sem("bias_ready"), sem("ex_ready"), sem("acc_step"), sem("gated"), sem("x_added")
        NACC = E1 + 1
        block = ctx.enter_context(nc.Block())

        @block.sync
        def _(sync):
            for dst, src in ((w_qkv, io.w_qkv), (b_qk, io.b_qk), (b_v, io.b_v), (w_gate, io.w_gate1), (b_gate, io.b_gate1),
                             (w_exp, io.w_exp), (b_exp, io.b_exp)):
                sync.dma_start(dst[:], src).then_inc(loaded, 16)
            with sync.Fori(0, B) as b:
                with sync.Fori(0, GPB) as q:
                    n = group_of(b, q)
                    store_values(sync, io, va, v_copied, v_stored, n, b, q)
                    split_store(sync, io, sp, n, b, q, paired=False)
            sync.wait_ge(v_stored, B * GPB * 16 * NHG)
            sync.wait_ge(sp.stored, B * GPB * 16 * 4 * NPART)

        @block.gpsimd
        def _(pool):
            nc.gpsimd.memset(va[:].rearrange("p t (h c) -> p (t h) c", c=AUG)[:, :, HD:AUG], 1.0).then_inc(ones_set, 1)

        @block.tensor
        def _(pe):
            pe.wait_ge(loaded, 7 * 16)
            with pe.Fori(0, B) as b:
                with pe.Fori(0, GPB) as q:
                    n = group_of(b, q)
                    pe.wait_ge(combT_copied, n)
                    pe.wait_ge(rt.step, n * ROUTE_STEPS)
                    ln_tensor(nc, pe, m, ln, n)
                    pe.wait_ge(ln.h_ready, n * KH + KH)
                    for t in range(TPG):
                        for kh in range(KH):
                            last = nc.tensor.matmul(logits_ps[:, t], ln.hT[:, kh, t * P:(t + 1) * P], w_gate[:, kh],
                                                    start=(kh == 0), stop=(kh == KH - 1))
                    last.then_inc(rt.logits_ready, 1)
                    pe.wait_ge(acc_step, n * TPG * NACC)
                    for a in range(4):
                        for kh in range(KH):
                            last = nc.tensor.matmul(qk_ps[:, a], w_qkv[:, kh, a * P:(a + 1) * P], ln.hT[:, kh],
                                                    start=(kh == 0), stop=(kh == KH - 1))
                        last.then_inc(qk_ready, 1)
                    for t in range(TPG):
                        for kh in range(KH):
                            last = nc.tensor.matmul(v_ps[:, t], ln.hT[:, kh, t * P:(t + 1) * P], w_qkv[:, kh, 2 * D:3 * D],
                                                    start=(kh == 0), stop=(kh == KH - 1))
                        if t % 2:
                            last.then_inc(v_ready, 1)
                    pe.wait_ge(comb_ready, n + 1)
                    for t in range(TPG):
                        last = nc.tensor.transpose(combT_ps[:, t], comb[:, t], m.ident[:])
                    last.then_inc(combT_ready, 1)
                    pe.wait_ge(combT_copied, n + 1)
                    pe.wait_ge(v_copied, n * 2 + 2)
                    for t in range(TPG):
                        last = nc.tensor.matmul(v_ps[:, t], combT[:, t], b_exp[:], start=True, stop=True)
                    last.then_inc(bias_ready, 1)
                    for t in range(TPG):
                        for pair in range(E1 // 2):
                            if t == 0:
                                pe.wait_ge(sp.whole_ready, n * 4 + pair + 1)
                            else:
                                pe.wait_ge(acc_step, (n * TPG + t - 1) * NACC + 1 + 2 * pair + 2)
                            for kh in range(KH):
                                last = nc.tensor.matmul(qk_ps[:, pair], ln.hT[:, kh, t * P:(t + 1) * P],
                                                        w_exp[:, kh, pair * 2 * D:(pair + 1) * 2 * D],
                                                        start=(kh == 0), stop=(kh == KH - 1))
                            last.then_inc(ex_ready, 1)

        @block.scalar
        def _(act):
            act.wait_ge(loaded, 7 * 16)
            act.wait_ge(ones_set, 1)
            with act.Fori(0, B) as b:
                with act.Fori(0, GPB) as q:
                    n = group_of(b, q)
                    ln_scalar(nc, act, m, ln, n, b, 1, 1, lambda: act.wait_ge(ex_ready, n * TPG * (E1 // 2)))
                    route_scalar(nc, act, rt, n)
                    act.wait_ge(sp.lo_ready, n * 4)
                    for a in range(4):
                        act.wait_ge(qk_ready, n * 4 + a + 1)
                        nc.scalar.activation(sp.whole[:, a], qk_ps[:, a], ACT.Identity, bias=b_qk[:, a:a + 1]).then_inc(sp.whole_ready, 1)
                    for a in range(4):
                        split_scalar_hi(nc, act, sp, n, a)
                    act.wait_ge(combT_ready, n + 1)
                    act.wait_ge(bias_ready, n)
                    nc.scalar.activation(combT[:], combT_ps, ACT.Copy).then_inc(combT_copied, 1)
                    for a in range(4):
                        split_scalar_mid(nc, act, sp, n, a)

        @block.vector
        def _(dve):
            dve.wait_ge(loaded, 7 * 16)
            dve.wait_ge(ones_set, 1)
            with dve.Fori(0, B) as b:
                with dve.Fori(0, GPB) as q:
                    n = group_of(b, q)
                    ln_vector(nc, dve, m, ln, n, lambda: None, None)
                    route_vector(nc, dve, m, rt, n, logits_ps, b_gate[:])
                    for k in range(2):
                        nc.vector.tensor_tensor(shares[:, k], rt.hot[:, k],
                                                rt.top[:, :, k:k + 1].broadcast_to([P, TPG, E1]), ALU.mult).then_inc(share_ready, 1)
                    dve.wait_ge(share_ready, n * 2 + 2)
                    nc.vector.tensor_tensor(comb[:], shares[:, 0], shares[:, 1], ALU.add).then_inc(comb_ready, 1)
                    dve.wait_ge(v_stored, n * (16 * NHG))
                    for pair in range(2):
                        dve.wait_ge(v_ready, n * 2 + pair + 1)
                        for t in (2 * pair, 2 * pair + 1):
                            ins = nc.vector.tensor_tensor(va[:, t].rearrange("p (h c) -> p h c", c=AUG)[:, :, 0:HD],
                                                          v_ps[:, t].rearrange("p (h c) -> p h c", c=HD),
                                                          b_v[:].rearrange("p (h c) -> p h c", c=HD), ALU.add)
                        ins.then_inc(v_copied, 1)
                    for a in range(4):
                        split_vector_rest(nc, dve, sp, n, a)
                    for a in range(4):
                        split_vector_lo(nc, dve, sp, n, a)
                    dve.wait_ge(comb_ready, n + 1)
                    dve.wait_ge(bias_ready, n + 1)
                    for t in range(TPG):
                        s = (n * TPG + t) * NACC
                        nc.vector.tensor_copy(acc[:, t], v_ps[:, t]).then_inc(acc_step, 1)
                        for e in range(E1):
                            if e % 2 == 0:
                                dve.wait_ge(ex_ready, (n * TPG + t) * (E1 // 2) + e // 2 + 1)
                            dve.wait_ge(acc_step, s + 1 + e)
                            nc.vector.scalar_tensor_tensor(acc[:, t], qk_ps[:, e // 2, (e % 2) * D:(e % 2 + 1) * D], comb[:, t, e:e + 1],
                                                           acc[:, t], ALU.mult, ALU.add).then_inc(acc_step, 1)
                    dve.wait_ge(acc_step, (n + 1) * TPG * NACC)
                    gate = m.gates[:, 1, 1, ds(b, 1)].broadcast_to([P, TPG, D])
                    nc.vector.tensor_tensor(acc_g[:], acc[:], gate, ALU.mult).then_inc(gated, 1)
                    dve.wait_ge(gated, n + 1)
                    xs = m.x[:, ds(n * TPG, TPG)]
                    nc.vector.tensor_tensor(xs, xs, acc_g[:], ALU.add).then_inc(x_added, 1)
                    dve.wait_ge(x_added, n + 1)


def add_attention_and_store(nc, m, io):
    with ExitStack() as ctx:
        sb, pb, sem = allocators(ctx, nc, "end")
        scaled = sb("scaled", [P, 2, TPG, D])
        y_scaled, y_added, out_stored = sem("y_scaled"), sem("y_added"), sem("out_stored")
        out = io.out.rearrange("(t p) d -> p t d", p=P)
        block = ctx.enter_context(nc.Block())

        @block.vector
        def _(dve):
            for n in range(B * GPB):
                b, q = n // GPB, n % GPB
                if n >= 2:
                    dve.wait_ge(y_added, n - 1)
                src = m.att[:, b, :, q * TPG:(q + 1) * TPG].rearrange("p g t c -> p t g c")
                for t in range(TPG):
                    ins = nc.vector.tensor_tensor(scaled[:, n % 2, t].rearrange("p (g c) -> p g c", g=NHG), src[:, t],
                                                  m.gates[:, 1, 1, b].rearrange("p (g c) -> p g c", g=NHG), ALU.mult)
                ins.then_inc(y_scaled, 1)
                dve.wait_ge(y_scaled, n + 1)
                xs = m.x[:, n * TPG:(n + 1) * TPG]
                nc.vector.tensor_tensor(xs, xs, scaled[:, n % 2], ALU.add).then_inc(y_added, 1)

        @block.sync
        def _(sync):
            for n in range(B * GPB):
                sync.wait_ge(y_added, n + 1)
                sync.dma_start(out[:, n * TPG:(n + 1) * TPG], m.x[:, n * TPG:(n + 1) * TPG]).then_inc(out_stored, 16)
            sync.wait_ge(out_stored, 16 * B * GPB)


class State:
    pass


def declare_state(nc, ctx):
    sb, _, sem = allocators(ctx, nc, "all")
    m = State()
    m.settled = sem("settled")
    m.x = sb("x_res", [P, NT, D])
    m.ident, m.ident_b = sb("ident", [P, P]), sb("ident_b", [P, P], BF16)
    m.triu, m.triu_b = sb("triu", [P, P]), sb("triu_b", [P, P], BF16)
    m.iota, m.eps = sb("iota", [P, E0]), sb("eps", [P, 1])
    m.modv = sb("modv", [P, 2, 4, KH, B])
    m.gates = sb("gates", [P, 2, 2, B, D])
    m.top_p, m.top_e = sb("top_p", [P, B, 2, TPB]), sb("top_e", [P, B, 2, TPB])
    m.chosen = sb("chosen", [P, B, 2, TPB, E0], BF16)
    return m


def build_program(nc, tensors, out):
    dram = lambda name, shape, dt=F32: nc.dram_tensor(name, shape, dt).ap()
    io = named(out=out, **tensors,
               q_parts=dram("q_parts", [NPART, B, NHG, HG, HD, T], BF16),
               k_parts=dram("k_parts", [NPART, B, NHG, HG, HD, T], BF16),
               v_rows=dram("v_rows", [B, NHG, P, TPB, VROW]),
               slot_rows=dram("slot_rows", [SLOTS, D]), slot_out=dram("slot_out", [SLOTS, D]))
    with ExitStack() as ctx:
        m = declare_state(nc, ctx)
        load_and_modulate(nc, m, io)
        project_layer0(nc, m, io)
        with nc.sbuf_tensor("z_all", [P, NT, D], F32) as z_all:
            m.z_all = z_all
            with nc.sbuf_tensor("att0", [P, B, NHG, TPB, HG * HD], F32) as att:
                m.att = att
                softmax_attention(nc, m, io, "att_l0")
                finish_attention0_and_route(nc, m, io)
            layer0_experts(nc, m, io)
        linear_attention(nc, m, io)
        project_layer1_ffn(nc, m, io)
        with nc.sbuf_tensor("att1", [P, B, NHG, TPB, HG * HD], F32) as att:
            m.att = att
            softmax_attention(nc, m, io, "att_l1")
            add_attention_and_store(nc, m, io)


def host_layout(inputs):
    f = lambda name: np.ascontiguousarray(inputs[name])
    halves = lambda w: np.ascontiguousarray(w.reshape(KH, P, -1).transpose(1, 0, 2))
    pairs = lambda w: w.reshape(NH, HD // 2, 2, D).transpose(2, 0, 1, 3).reshape(D, D)
    pos = np.arange(T, dtype=np.float32)[None, :]
    freq = np.exp(np.float32(-np.log(10000.0)) * np.arange(0, HD, 2, dtype=np.float32) / np.float32(HD)).astype(np.float32)
    angle = np.tile(freq, NH)[:, None] * pos
    pi = np.arange(P)
    out = {
        "x": f("L0_attn_x").reshape(B * T, D),
        "c_t": np.stack([f("L0_c").T.reshape(KH, P, B), f("L1_c").T.reshape(KH, P, B)]).transpose(2, 0, 1, 3),
        "wmod": np.stack([halves(f("L0_wmod")), halves(f("L1_wmod"))], axis=1),
        "l0_wqk": halves(np.concatenate([pairs(f("L0_attn_W_q")), pairs(f("L0_attn_W_k"))]).T),
        "l0_wv": halves(f("L0_attn_W_v").T),
        "l0_wo": halves(f("L0_attn_W_o").T),
        "w_router": halves(f("L0_ffn_w_router")),
        "w_gate_fc": np.concatenate([f("L0_ffn_w_gate").reshape(E0, KH, P, HID), f("L0_ffn_w_fc").reshape(E0, KH, P, HID)],
                                    axis=3).transpose(0, 2, 1, 3),
        "w_proj": f("L0_ffn_w_proj"),
        "l1_wqk": halves(np.concatenate([f("L1_attn_Wq"), f("L1_attn_Wk")]).T),
        "l1_wkv": halves(np.concatenate([f("L1_attn_Wk"), f("L1_attn_Wv")]).T),
        "l1_wo": halves(f("L1_attn_Wo").T),
        "w_qkv": halves(f("L1_ffn_W_qkv")),
        "b_qk": f("L1_ffn_b_qkv")[:2 * D].reshape(4, P).T,
        "b_v": np.broadcast_to(f("L1_ffn_b_qkv")[2 * D:], (P, D)),
        "w_gate1": halves(f("L1_ffn_W_gate")),
        "b_gate1": np.broadcast_to(f("L1_ffn_b_gate"), (P, E1)),
        "w_exp": halves(f("L1_ffn_W_experts").transpose(1, 0, 2).reshape(D, E1 * D)),
        "b_exp": f("L1_ffn_b_experts"),
        "ident": np.eye(P, dtype=np.float32),
        "triu": (pi[:, None] <= pi[None, :]).astype(np.float32),
        "iota": np.tile(np.arange(E0, dtype=np.float32), (P, 1)),
        "head_of": (pi[:, None] // HD == np.arange(NHH)[None, :]).astype(np.float32),
        "cos": np.cos(angle).astype(np.float32),
        "sin": np.sin(angle).astype(np.float32),
    }
    return {k: np.ascontiguousarray(v) for k, v in out.items()}


def kernel(**inputs):
    import concourse.bacc as _bacc
    from concourse.bass_utils import run_bass_kernel_spmd as _run

    nc = _bacc.Bacc("TRN2", target_bir_lowering=False, num_devices=1)
    arrays = host_layout({k: np.asarray(v) for k, v in inputs.items()})
    tensors = {name: nc.dram_tensor(f"in_{name}", a.shape, mybir.dt.from_np(a.dtype), kind="ExternalInput").ap()
               for name, a in arrays.items()}
    build_program(nc, tensors, nc.dram_tensor("out", [B * T, D], F32, kind="ExternalOutput").ap())
    r = _run(nc, [{f"in_{k}": v for k, v in arrays.items()}], core_ids=[0])
    return r.results[0]["out"].reshape(B, T, D)
```

```python
from collections import namedtuple
from contextlib import ExitStack

import numpy as np

import concourse.bass as bass
from concourse import mybir

ALU = mybir.AluOpType
ACT = mybir.ActivationFunctionType
AX = mybir.AxisListType
F32 = mybir.dt.float32
BF16 = mybir.dt.bfloat16
I32 = mybir.dt.int32
U32 = mybir.dt.uint32
ds = bass.ds

P = 128
B, T, D = 2, 2048, 256
NH, HD = 16, 16
NT = B * T // P
TPB = T // P
G = 512
TPG = G // P
GPB = T // G
KH = D // P
HG = 4
NHG = NH // HG
AUG = HD + 1
VROW = HG * AUG
NPART = 3
QPART = (0, 0, 1, 0, 2, 1)
KPART = (0, 1, 0, 2, 0, 1)
SROWS = HD * len(QPART)
XROWS = SROWS + NPART
E0, CAP = 16, 256
SLOTS = E0 * B * CAP
E1 = 8
HID = 128
EPS_LN, EPS_LIN = 1e-5, 1e-6
HALF = D // 2
NHH = NH // KH


def named(**things):
    return namedtuple("Named", things)(**things)


def allocators(ctx, nc, tag):
    sems = []

    def semaphore(name):
        sems.append(nc.alloc_semaphore(f"{tag}_{name}"))
        return sems[-1]

    def clear():
        if sems:
            nc.clear_and_free_semaphores(sems)
            nc.all_engine_barrier()

    ctx.callback(clear)
    return (lambda name, shape, dt=F32: ctx.enter_context(nc.sbuf_tensor(f"{tag}_{name}", shape, dt)),
            lambda name, shape, dt=F32: ctx.enter_context(nc.psum_tensor(f"{tag}_{name}", shape, dt)),
            semaphore)


def settle(eng, m):
    eng.sem_inc(m.settled, 1)


def group_of(b, q):
    return b * GPB + q


def next_group(b, q):
    n = (group_of(b, q) + 1) % (B * GPB)
    return n // GPB, n * TPG


def load_and_modulate(nc, m, io):
    with ExitStack() as ctx:
        sb, pb, sem = allocators(ctx, nc, "mod")
        wmod = sb("wmod", [P, 2, KH, 6 * D])
        cT = sb("cT", [P, 2, KH, B])
        sig = sb("sig", [P, 2, KH, B])
        cs = sb("cs", [P, 2 * KH * B])
        cs_rows = sb("cs_rows", [P, 2 * KH * B, P])
        gsign = sb("gsign", [P, 2, 2 * B * D])
        cols = pb("mod_cols", [P, 512])
        rows = pb("mod_rows", [P, 2 * B, 512])
        consts_loaded, c_loaded, w_loaded = sem("consts_loaded"), sem("c_loaded"), sem("w_loaded")
        c_exp, c_step, silu_ready, rows_ready = sem("c_exp"), sem("c_step"), sem("silu_ready"), sem("rows_ready")
        cols_done, gates_done, mod_step = sem("cols_done"), sem("gates_done"), sem("mod_step")
        block = ctx.enter_context(nc.Block())

        @block.sync
        def _(sp):
            sp.dma_start(cT[:], io.c_t).then_inc(c_loaded, 16)
            sp.dma_start(wmod[:, 0], io.wmod[:, 0]).then_inc(w_loaded, 16)
            sp.dma_start(wmod[:, 1], io.wmod[:, 1]).then_inc(w_loaded, 16)
            xt = io.x.rearrange("(t p) d -> p t d", p=P)
            sp.dma_start(m.ident[:], io.ident).then_inc(consts_loaded, 16)
            sp.dma_start(m.triu[:], io.triu).then_inc(consts_loaded, 16)
            sp.dma_start(m.iota[:], io.iota).then_inc(consts_loaded, 16)
            for b in range(B):
                sp.dma_start(m.x[:, b * TPB:(b + 1) * TPB], xt[:, b * TPB:(b + 1) * TPB]).then_inc(m.x_loaded[b], 16)

        @block.scalar
        def _(act):
            act.wait_ge(c_loaded, 16)
            nc.scalar.activation(sig[:], cT[:], ACT.Exp, scale=-1.0).then_inc(c_exp, 1)

        @block.tensor
        def _(pe):
            pe.wait_ge(silu_ready, 2)
            pe.wait_ge(w_loaded, 32)
            last = None
            for layer in range(2):
                for v, idx in enumerate((0, 1, 3, 4)):
                    for half in range(KH):
                        o = ((layer * 4 + v) * KH + half) * B
                        for kh in range(KH):
                            c0 = idx * D + half * P
                            k0 = (layer * KH + kh) * B
                            last = nc.tensor.matmul(cols[:, o:o + B], wmod[:, layer, kh, c0:c0 + P],
                                                    cs[:, k0:k0 + B], start=(kh == 0), stop=(kh == KH - 1))
            last.then_inc(cols_done, 1)
            for layer in range(2):
                for v, idx in enumerate((2, 5)):
                    for b in range(B):
                        o = b * D
                        for kh in range(KH):
                            last = nc.tensor.matmul(rows[:, layer * 2 + v, o:o + D],
                                                    cs_rows[:, (layer * KH + kh) * B + b, :],
                                                    wmod[:, layer, kh, idx * D:(idx + 1) * D],
                                                    start=(kh == 0), stop=(kh == KH - 1))
            last.then_inc(rows_ready, 1)

        @block.vector
        def _(dve):
            dve.wait_ge(c_exp, 1)
            sg = sig[:].rearrange("p a b c -> p (a b c)")
            nc.vector.tensor_scalar(sg, sg, 1.0, None, ALU.add).then_inc(c_step, 1)
            dve.wait_ge(c_step, 1)
            nc.vector.reciprocal(sg, sg).then_inc(c_step, 1)
            dve.wait_ge(c_step, 2)
            nc.vector.tensor_tensor(cs[:], sg, cT[:].rearrange("p a b c -> p (a b c)"), ALU.mult).then_inc(silu_ready, 1)
            dve.wait_ge(silu_ready, 1)
            nc.vector.tensor_copy(cs_rows[:], cs[:].unsqueeze(2).broadcast_to([P, 2 * KH * B, P])).then_inc(silu_ready, 1)
            dve.wait_ge(consts_loaded, 48)
            nc.vector.tensor_copy(m.ident_b[:], m.ident[:])
            nc.vector.tensor_copy(m.triu_b[:], m.triu[:])
            nc.vector.memset(m.eps[:], EPS_LN)
            dve.wait_ge(cols_done, 1)
            cv = cols[:, 0:16 * B].rearrange("p (l v r) -> p l v r", l=2, v=4)
            mv = m.modv[:].rearrange("p l v h b -> p l v (h b)")
            for v in (0, 2):
                nc.vector.tensor_copy(mv[:, :, v], cv[:, :, v])
                nc.vector.tensor_scalar(mv[:, :, v + 1], cv[:, :, v + 1], 1.0, None, ALU.add)
            dve.wait_ge(rows_ready, 1)
            for layer in range(2):
                rv = rows[:, layer * 2:layer * 2 + 2].rearrange("p a n -> p (a n)")
                gv = m.gates[:, layer].rearrange("p a b d -> p (a b d)")
                nc.vector.tensor_scalar(gsign[:, layer], rv, 0.0, 2.0, ALU.is_ge, ALU.mult).then_inc(mod_step, 1)
                dve.wait_ge(mod_step, 3 * layer + 1)
                nc.vector.tensor_scalar(gsign[:, layer], gsign[:, layer], -1.0, None, ALU.add).then_inc(mod_step, 1)
                dve.wait_ge(mod_step, 3 * layer + 2)
                nc.vector.tensor_tensor(gv, rv, gsign[:, layer], ALU.mult).then_inc(mod_step, 1)
                dve.wait_ge(mod_step, 3 * layer + 3)
                nc.vector.scalar_tensor_tensor(gv, gv, 0.25, gsign[:, layer], ALU.max, ALU.mult).then_inc(gates_done, 1)
            dve.wait_ge(gates_done, 2)


def ln_buffers(ctx, nc, tag, ring=1):
    sb, pb, sem = allocators(ctx, nc, tag)
    return named(
        stats=sb("ln_stats", [P, TPG, 6]), mv=sb("ln_mv", [P, TPG, 2]), std=sb("ln_std", [P, TPG]),
        rstd=sb("ln_rstd", [P, TPG]), z=sb("ln_z", [P, TPG, D]), hT=sb("ln_hT", [P, ring * KH, G]),
        zT=pb("ln_zT", [P, KH, G]),
        stats_done=sem("ln_stats_done"), var_ready=sem("ln_var_ready"), std_ready=sem("ln_std_ready"),
        rstd_ready=sem("ln_rstd_ready"), z_ready=sem("ln_z_ready"), zT_ready=sem("ln_zT_ready"),
        h_ready=sem("ln_h_ready"))


def ln_stats(nc, dve, m, ln, n, tile):
    settle(dve, m)
    for t in range(TPG):
        nc.vector.bn_stats(ln.stats[:, t], m.x[:, ds(tile + t, 1)].rearrange("p a d -> p (a d)")).then_inc(ln.stats_done, 1)
    dve.wait_ge(ln.stats_done, n * TPG + TPG)
    settle(dve, m)
    for t in range(TPG):
        nc.vector.bn_aggr(ln.mv[:, t], ln.stats[:, t]).then_inc(ln.var_ready, 1)


def ln_normalize(nc, dve, m, ln, n, tile, z_free):
    dve.wait_ge(ln.std_ready, n + 1)
    nc.vector.reciprocal(ln.rstd[:], ln.std[:]).then_inc(ln.rstd_ready, 1)
    dve.wait_ge(ln.rstd_ready, n + 1)
    dve.wait_ge(ln.zT_ready, n)
    z_free()
    for t in range(TPG):
        nc.vector.tensor_scalar(ln.z[:, t], m.x[:, ds(tile + t, 1)].rearrange("p a d -> p (a d)"),
                                ln.mv[:, t, 0:1], ln.rstd[:, t:t + 1], ALU.subtract, ALU.mult).then_inc(ln.z_ready, 1)


def ln_tensor(nc, pe, m, ln, n):
    pe.wait_ge(ln.h_ready, n * KH)
    for t in range(TPG):
        pe.wait_ge(ln.z_ready, n * TPG + t + 1)
        for half in range(KH):
            last = nc.tensor.transpose(ln.zT[:, half, t * P:(t + 1) * P], ln.z[:, t, half * P:(half + 1) * P], m.ident[:])
    last.then_inc(ln.zT_ready, 1)


def ln_root(nc, act, m, ln, n):
    act.wait_ge(ln.var_ready, n * TPG + TPG)
    nc.scalar.activation(ln.std[:], ln.mv[:, :, 1], ACT.Sqrt, bias=m.eps[:, 0:1]).then_inc(ln.std_ready, 1)


def ln_shift(nc, act, m, ln, n, b, layer, which, h_free=lambda: None, slot=0):
    act.wait_ge(ln.zT_ready, n + 1)
    h_free()
    for half in range(KH):
        shift = m.modv[:, layer, 2 * which, half, ds(b, 1)]
        scale = m.modv[:, layer, 2 * which + 1, half, ds(b, 1)]
        dst = ln.hT[:, ds(slot * KH + half, 1)].rearrange("p a n -> p (a n)")
        nc.scalar.activation(dst, ln.zT[:, half], ACT.Identity, bias=shift, scale=scale).then_inc(ln.h_ready, 1)


def split_buffers(ctx, nc, tag):
    sb, pb, sem = allocators(ctx, nc, tag)
    return named(
        whole=sb("sp_whole", [P, 4, G]), rest=sb("sp_rest", [P, 4, G]), parts=sb("sp_parts", [P, 4, NPART, G], BF16),
        whole_ready=sem("sp_whole_ready"), hi_ready=sem("sp_hi_ready"), rest_ready=sem("sp_rest_ready"),
        mid_ready=sem("sp_mid_ready"), lo_ready=sem("sp_lo_ready"), stored=sem("sp_stored"))


def split_scalar_hi(nc, act, sp, n, a):
    act.wait_ge(sp.whole_ready, n * 4 + a + 1)
    act.wait_ge(sp.stored, n * (16 * 4 * NPART))
    nc.scalar.activation(sp.parts[:, a, 0], sp.whole[:, a], ACT.Copy).then_inc(sp.hi_ready, 1)


def split_vector_rest(nc, dve, sp, n, a):
    dve.wait_ge(sp.hi_ready, n * 4 + a + 1)
    nc.vector.tensor_tensor(sp.rest[:, a], sp.whole[:, a], sp.parts[:, a, 0], ALU.subtract).then_inc(sp.rest_ready, 1)


def split_scalar_mid(nc, act, sp, n, a):
    act.wait_ge(sp.rest_ready, n * 4 + a + 1)
    nc.scalar.activation(sp.parts[:, a, 1], sp.rest[:, a], ACT.Copy).then_inc(sp.mid_ready, 1)


def split_vector_lo(nc, dve, sp, n, a):
    dve.wait_ge(sp.mid_ready, n * 4 + a + 1)
    nc.vector.tensor_tensor(sp.parts[:, a, 2], sp.rest[:, a], sp.parts[:, a, 1], ALU.subtract).then_inc(sp.lo_ready, 1)


def split_store(sync, io, sp, n, b, q, paired):
    for a in range(4):
        sync.wait_ge(sp.lo_ready, n * 4 + a + 1)
        dram = (io.q_parts, io.k_parts)[a // 2]
        r = a % 2
        for part in range(NPART):
            rows = dram[part, ds(b, 1)].rearrange("a g h c t -> (a g h) c t")[:, :, ds(q * G, G)]
            if paired:
                dst = rows[:, r * (HD // 2):(r + 1) * (HD // 2)]
                src = sp.parts[:, a, part]
            else:
                dst = rows[r * NHH:(r + 1) * NHH].rearrange("h c t -> (h c) t")
                src = sp.parts[:, a, part]
            sync.dma_start(dst, src).then_inc(sp.stored, 16)


def store_values(sync, io, va, v_copied, v_stored, n, b, q):
    sync.wait_ge(v_copied, n * 2 + 2)
    for g in range(NHG):
        dst = io.v_rows[ds(b, 1), g].rearrange("a p t n -> (a p) t n")[:, ds(q * TPG, TPG)]
        sync.dma_start(dst, va[:, :, g * VROW:(g + 1) * VROW]).then_inc(v_stored, 16)


def project_layer0(nc, m, io):
    with ExitStack() as ctx:
        sb, pb, sem = allocators(ctx, nc, "qkv0")
        ln, sp = ln_buffers(ctx, nc, "qkv0", ring=2), split_buffers(ctx, nc, "qkv0")
        w_qk = sb("w_qk", [P, KH, 4 * P])
        w_v = sb("w_v", [P, KH, D])
        cos, sin = sb("cos", [P, T]), sb("sin", [P, T])
        prod = sb("prod", [P, 4, G])
        va = sb("va", [P, TPG, NH * AUG])
        qk_ps = pb("qk_ps", [P, 4, G])
        v_ps = pb("v_ps", [P, TPG, D])
        loaded, ones_set = sem("loaded"), sem("ones_set")
        qk_ready, v_ready, v_copied, v_stored = sem("qk_ready"), sem("v_ready"), sem("v_copied"), sem("v_stored")
        prod_ready = sem("prod_ready")
        block = ctx.enter_context(nc.Block())

        @block.sync
        def _(sync):
            sync.dma_start(w_qk[:], io.l0_wqk).then_inc(loaded, 16)
            sync.dma_start(w_v[:], io.l0_wv).then_inc(loaded, 16)
            sync.dma_start(cos[:], io.cos).then_inc(loaded, 16)
            sync.dma_start(sin[:], io.sin).then_inc(loaded, 16)
            with sync.Fori(0, B) as b:
                with sync.Fori(0, GPB) as q:
                    n = group_of(b, q)
                    store_values(sync, io, va, v_copied, v_stored, n, b, q)
                    split_store(sync, io, sp, n, b, q, paired=True)
            sync.wait_ge(v_stored, B * GPB * 16 * NHG)
            sync.wait_ge(sp.stored, B * GPB * 16 * 4 * NPART)

        @block.gpsimd
        def _(pool):
            nc.gpsimd.memset(va[:].rearrange("p t (h c) -> p (t h) c", c=AUG)[:, :, HD:AUG], 1.0).then_inc(ones_set, 1)

        @block.vector
        def _(dve):
            dve.wait_ge(m.x_loaded[0], 16)
            ln_stats(nc, dve, m, ln, 0, 0)
            ln_normalize(nc, dve, m, ln, 0, 0, lambda: None)
            dve.wait_ge(loaded, 64)
            dve.wait_ge(m.x_loaded[1], 16)
            with dve.Fori(0, B) as b:
                with dve.Fori(0, GPB) as q:
                    n = group_of(b, q)
                    _, tile = next_group(b, q)
                    ln_stats(nc, dve, m, ln, n + 1, tile)
                    ln_normalize(nc, dve, m, ln, n + 1, tile, lambda: None)
                    c, s = cos[:, ds(q * G, G)], sin[:, ds(q * G, G)]
                    for a in range(2):
                        dve.wait_ge(qk_ready, n * 4 + 2 * a + 2)
                        dve.wait_ge(sp.whole_ready, n * 4 + 2 * a)
                        for r, (src, by) in enumerate(((0, c), (1, s), (0, s), (1, c))):
                            nc.vector.tensor_tensor(prod[:, r], qk_ps[:, 2 * a + src], by, ALU.mult).then_inc(prod_ready, 1)
                        dve.wait_ge(prod_ready, n * 8 + 4 * a + 4)
                        dve.wait_ge(sp.lo_ready, n * 4)
                        nc.vector.tensor_tensor(sp.whole[:, 2 * a], prod[:, 0], prod[:, 1], ALU.subtract).then_inc(sp.whole_ready, 1)
                        nc.vector.tensor_tensor(sp.whole[:, 2 * a + 1], prod[:, 2], prod[:, 3], ALU.add).then_inc(sp.whole_ready, 1)
                    for a in range(4):
                        split_vector_rest(nc, dve, sp, n, a)
                    for a in range(4):
                        split_vector_lo(nc, dve, sp, n, a)

        @block.scalar
        def _(act):
            act.wait_ge(ones_set, 1)
            ln_root(nc, act, m, ln, 0)
            ln_shift(nc, act, m, ln, 0, 0, 0, 0)
            with act.Fori(0, B) as b:
                with act.Fori(0, GPB) as q:
                    n = group_of(b, q)
                    b_next, _ = next_group(b, q)
                    ln_root(nc, act, m, ln, n + 1)
                    for a in range(2):
                        split_scalar_hi(nc, act, sp, n, a)
                    ln_shift(nc, act, m, ln, n + 1, b_next, 0, 0, lambda: act.wait_ge(v_ready, n * 2), (n + 1) % 2)
                    act.wait_ge(v_stored, n * (16 * NHG))
                    for pair in range(2):
                        act.wait_ge(v_ready, n * 2 + pair + 1)
                        dst = va[:, 2 * pair:2 * pair + 2].rearrange("p t (h c) -> p t h c", c=AUG)[:, :, :, 0:HD]
                        src = v_ps[:, 2 * pair:2 * pair + 2].rearrange("p t (h c) -> p t h c", c=HD)
                        nc.scalar.activation(dst, src, ACT.Copy).then_inc(v_copied, 1)
                    for a in range(2, 4):
                        split_scalar_hi(nc, act, sp, n, a)
                    for a in range(4):
                        split_scalar_mid(nc, act, sp, n, a)

        @block.tensor
        def _(pe):
            ln_tensor(nc, pe, m, ln, 0)
            pe.wait_ge(loaded, 64)
            with pe.Fori(0, B * GPB // 2) as i:
                for slot in range(2):
                    n = 2 * i + slot
                    h = ln.hT[:, slot * KH:(slot + 1) * KH]
                    pe.wait_ge(ln.h_ready, n * KH + KH)
                    pe.wait_ge(prod_ready, n * 8)
                    for a in range(4):
                        for kh in range(KH):
                            last = nc.tensor.matmul(qk_ps[:, a], w_qk[:, kh, a * P:(a + 1) * P], h[:, kh],
                                                    start=(kh == 0), stop=(kh == KH - 1))
                        last.then_inc(qk_ready, 1)
                    ln_tensor(nc, pe, m, ln, n + 1)
                    pe.wait_ge(v_copied, n * 2)
                    for t in range(TPG):
                        for kh in range(KH):
                            last = nc.tensor.matmul(v_ps[:, t], h[:, kh, t * P:(t + 1) * P], w_v[:, kh],
                                                    start=(kh == 0), stop=(kh == KH - 1))
                        if t % 2:
                            last.then_inc(v_ready, 1)


NG = NHG
NB = GPB * NG
KT = TPB
TURN_AT = (13, 14)
COPY_AT = (13, 13, 14, 14)
LEAD = 6
MAXI = HG * TPG * 2


ZEROS = 2048


def softmax_attention(nc, m, io, tag, zero_slots=False):
    with ExitStack() as ctx:
        sb, pb, sem = allocators(ctx, nc, tag)
        QR = 4
        q_sb = sb("q_sb", [P, QR, HG, G], BF16)
        k_sb = sb("k_sb", [P, 2, HG, T], BF16)
        v_sb = sb("v_sb", [P, 2, TPB, VROW])
        probs = sb("probs", [P, 2, HG, G])
        part_max = sb("part_max", [P, 2, MAXI])
        row_max = sb("row_max", [P, HG * TPG])
        max_rest = sb("max_rest", [P, HG * TPG])
        max_parts = sb("max_parts", [P, HG * TPG, NPART], BF16)
        o_sb = sb("o_sb", [P, G])
        inv = sb("inv", [P, TPG, HG])
        s_ps = pb("s_ps", [P, 2, G])
        max_ps = pb("max_ps", [P, 2, 2, G])
        o_ps = pb("o_ps", [P, G])
        turn_ps = pb("turn_ps", [P, TPG, P])
        turn_b = turn_ps[:].rearrange("p a b -> p (a b)").bitcast(BF16)
        q_loaded = [sem(f"q_loaded{r}") for r in range(QR)]
        k_loaded = [sem(f"k_loaded{r}") for r in range(2)]
        v_loaded = [sem(f"v_loaded{r}") for r in range(2)]
        rows_set, o_zeroed = sem("rows_set"), sem("o_zeroed")
        s_ready, exp_done, pv_done = sem("s_ready"), sem("exp_done"), sem("pv_done")
        maxs_ready, max_taken = sem("maxs_ready"), sem("max_taken")
        rowmax_step, parts_ready, maxT_ready, maxT_copied = sem("rowmax_step"), sem("parts_ready"), sem("maxT_ready"), sem("maxT_copied")
        o_copied, turned, inv_ready, att_done = sem("o_copied"), sem("turned"), sem("inv_ready"), sem("att_done")
        zeros = sb("zeros", [P, ZEROS])
        zero_ready, slots_zeroed = sem("zero_ready"), sem("slots_zeroed")
        NIT = B * NHG // NG
        att = m.att[:].rearrange("p b (i g) t n -> p (b i) g t n", g=NG)
        kd = io.k_parts.rearrange("s b (i g) h c t -> s (b i) g c h t", g=NG)
        qd = io.q_parts.rearrange("s b (i g) h c t -> s (b i) g c h t", g=NG)
        vd = io.v_rows.rearrange("b (i g) p t n -> (b i) g p t n", g=NG)
        block = ctx.enter_context(nc.Block())

        def load_q(eng, it, j):
            for r, part in enumerate(QPART):
                src = qd[part, ds(it, 1), j // GPB].rearrange("a c h t -> (a c) h t")
                eng.dma_start(q_sb[r * HD:(r + 1) * HD, j % QR],
                              src[:, :, (j % GPB) * G:(j % GPB + 1) * G]).then_inc(q_loaded[j % QR], 16)

        def load_k(eng, it, g):
            for r, part in enumerate(KPART):
                src = kd[part, ds(it, 1), g].rearrange("a c h t -> (a c) h t")
                eng.dma_start(k_sb[r * HD:(r + 1) * HD, g % 2], src).then_inc(k_loaded[g % 2], 16)

        def load_v(eng, it, g):
            eng.dma_start(v_sb[:, g % 2], vd[ds(it, 1), g].rearrange("a p t n -> (a p) t n")).then_inc(v_loaded[g % 2], 16)

        NQ, NK = 16 * len(QPART), 16 * len(KPART)

        @block.sync
        def _(sync):
            load_q(sync, 0, 0)
            load_k(sync, 0, 0)
            for j in (1, 2):
                load_q(sync, 0, j)
            load_v(sync, 0, 0)
            with sync.Fori(0, NIT) as it:
                ahead = (it + 1) % NIT
                for j in range(NB):
                    n = it * NB + j
                    sync.wait_ge(exp_done, n * (KT * HG))
                    load_q(sync, it if j + 3 < NB else ahead, (j + 3) % NB)
                    if j % GPB == 0:
                        g = j // GPB + 1
                        load_k(sync, it if g < NG else ahead, g % NG)
                        sync.wait_ge(pv_done, n * KT)
                        load_v(sync, it if g < NG else ahead, g % NG)
            for r in range(QR):
                sync.wait_ge(q_loaded[r], NQ * (B * NHG * GPB // QR + (r < 3)))
            for g in range(2):
                sync.wait_ge(k_loaded[g], NK * (NIT * NG // 2 + (g == 0)))
                sync.wait_ge(v_loaded[g], 16 * (NIT * NG // 2 + (g == 0)))

        @block.gpsimd
        def _(pool):
            nc.gpsimd.memset(k_sb[SROWS:XROWS], -1.0).then_inc(rows_set, 1)
            if zero_slots:
                pool.wait_ge(rows_set, 1)
                nc.gpsimd.memset(zeros[:], 0.0).then_inc(zero_ready, 1)
                pool.wait_ge(zero_ready, 1)
                pool.wait_ge(exp_done, KT * HG)
                flat = io.slot_rows.rearrange("(p n) d -> p (n d)", p=P)
                for k in range(SLOTS * D // P // ZEROS):
                    pool.dma_start(flat[:, k * ZEROS:(k + 1) * ZEROS], zeros[:]).then_inc(slots_zeroed, 16)
                pool.wait_ge(slots_zeroed, 16 * (SLOTS * D // P // ZEROS))

        def max_scores(pe, n, j, k, it2):
            if k == 0:
                pe.wait_ge(q_loaded[j % QR], NQ * (it2 * (NB // QR) + j // QR + 1))
                if j % GPB == 0:
                    g = j // GPB
                    pe.wait_ge(k_loaded[g % 2], NK * (it2 * (NG // 2) + g // 2 + 1))
            head, tile, half = k // (2 * TPG), k // 2 % TPG, k % 2
            if not (isinstance(n, int) and n * MAXI + k < 2):
                pe.wait_ge(max_taken, n * MAXI + k - 1)
            for c in range(2):
                last = nc.tensor.matmul(max_ps[:, k % 2, c], q_sb[0:SROWS, j % QR, head, tile * P:(tile + 1) * P],
                                        k_sb[0:SROWS, j // GPB % 2, head, (2 * half + c) * G:(2 * half + c + 1) * G],
                                        start=True, stop=True)
                if c == 0:
                    yield
            last.then_inc(maxs_ready, 1)
            yield

        def max_take(dve, n, j, k):
            dve.wait_ge(maxs_ready, n * MAXI + k + 1)
            nc.vector.reduce_max(part_max[:, j % 2, k:k + 1], max_ps[:, k % 2].rearrange("p a n -> p (a n)"), AX.X).then_inc(max_taken, 1)

        def row_maxima(dve, n, j, s):
            if s == 0:
                dve.wait_ge(max_taken, (n + 1) * MAXI)
                nc.vector.reduce_max(row_max[:], part_max[:, j % 2].rearrange("p (a h) -> p a h", h=2), AX.X).then_inc(rowmax_step, 1)
            elif s == 1:
                dve.wait_ge(rowmax_step, n * 4 + 1)
                dve.wait_ge(maxT_ready, n * 2)
                nc.vector.tensor_copy(max_parts[:, :, 0], row_max[:]).then_inc(rowmax_step, 1)
            elif s == 2:
                dve.wait_ge(rowmax_step, n * 4 + 2)
                nc.vector.tensor_tensor(max_rest[:], row_max[:], max_parts[:, :, 0], ALU.subtract).then_inc(rowmax_step, 1)
            elif s == 3:
                dve.wait_ge(rowmax_step, n * 4 + 3)
                nc.vector.tensor_copy(max_parts[:, :, 1], max_rest[:]).then_inc(rowmax_step, 1)
            elif s == 4:
                dve.wait_ge(rowmax_step, n * 4 + 4)
                nc.vector.tensor_tensor(max_parts[:, :, 2], max_rest[:], max_parts[:, :, 1], ALU.subtract).then_inc(parts_ready, 1)

        def turn_maxima(pe, n, r):
            if r == 0:
                pe.wait_ge(parts_ready, n + 1)
                if not isinstance(n, int):
                    pe.wait_ge(att_done, n - 1)
            pe.wait_ge(maxT_copied, n * HG + 2 * r)
            for i in range(2 * TPG):
                last = nc.tensor.transpose(turn_b[SROWS:XROWS, i * P:(i + 1) * P],
                                           max_parts[:, r * 2 * TPG + i], m.ident_b[:])
            last.then_inc(maxT_ready, 1)

        def copy_maxima(act, n, j, h):
            act.wait_ge(maxT_ready, n * 2 + h // 2 + 1)
            nc.scalar.activation(q_sb[SROWS:XROWS, j % QR, h], turn_b[SROWS:XROWS, h % 2 * G:(h % 2 + 1) * G],
                                 ACT.Copy).then_inc(maxT_copied, 1)

        @block.tensor
        def _(pe):
            def items(n, j, ks, it2):
                for k in ks:
                    yield from max_scores(pe, n, j, k, it2)

            def scores(n, j, u, h):
                c = (n * KT + u) * HG + h
                if u == 0 and h == 0:
                    pe.wait_ge(maxT_copied, n * HG + HG)
                    if j == 0:
                        pe.wait_ge(exp_done, c)
                if not (u == 0 and h == 0 and j == 0):
                    pe.wait_ge(exp_done, c - 1)
                nc.tensor.matmul(s_ps[:, h % 2], k_sb[0:XROWS, j // GPB % 2, h, u * P:(u + 1) * P],
                                 q_sb[0:XROWS, j % QR, h], start=True, stop=True).then_inc(s_ready, 1)

            def values(n, j, u, it):
                pe.wait_ge(exp_done, (n * KT + u + 1) * HG)
                if u == 0:
                    pe.wait_ge(o_copied, n)
                    if j % GPB == 0:
                        g = j // GPB
                        pe.wait_ge(v_loaded[g % 2], 16 * (it * (NG // 2) + g // 2 + 1))
                for h in range(HG):
                    last = nc.tensor.matmul(o_ps[32 * h:32 * h + AUG], v_sb[:, j // GPB % 2, u, h * AUG:(h + 1) * AUG],
                                            probs[:, u % 2, h], start=(u == 0), stop=(u == KT - 1))
                last.then_inc(pv_done, 1)

            def turn_result(n):
                pe.wait_ge(o_copied, n + 1)
                for t in range(TPG):
                    last = nc.tensor.transpose(turn_ps[:, t], o_sb[:, t * P:(t + 1) * P], m.ident[:])
                last.then_inc(turned, 1)

            pe.wait_ge(o_zeroed, 1)
            for _ in items(0, 0, range(MAXI), 0):
                pass
            for _ in items(1, 1, range(2 * LEAD), 0):
                pass
            for r in range(2):
                turn_maxima(pe, 0, r)
            pe.wait_ge(rows_set, 1)
            with pe.Fori(0, NIT) as it:
                for j in range(NB):
                    n = it * NB + j
                    for u in range(KT):
                        k = 2 * (u + LEAD)
                        ahead = 1 + k // MAXI
                        share = items(n + ahead, (j + ahead) % NB, (k % MAXI, k % MAXI + 1),
                                      it + (j + ahead) // NB)
                        if u == 2 and j > 0:
                            turn_result(n - 1)
                        scores(n, j, u, 0)
                        scores(n, j, u, 1)
                        if u > 0:
                            values(n, j, u - 1, it)
                        elif j > 0:
                            values(n - 1, j - 1, KT - 1, it)
                        scores(n, j, u, 2)
                        next(share)
                        scores(n, j, u, 3)
                        if u in TURN_AT:
                            turn_maxima(pe, n + 1, TURN_AT.index(u))
                        next(share)
                        next(share)
                        next(share)
                values(n, NB - 1, KT - 1, it)
                pe.wait_ge(maxT_copied, (n + 2) * HG)
                turn_result(n)

        @block.scalar
        def _(act):
            def exps(n, u, h):
                c = (n * KT + u) * HG + h
                act.wait_ge(s_ready, c + 1)
                nc.scalar.activation(probs[:, u % 2, h], s_ps[:, h % 2], ACT.Exp, scale=float(HD) ** -0.5).then_inc(exp_done, 1)

            def copy_result(n):
                act.wait_ge(pv_done, (n + 1) * KT)
                act.wait_ge(turned, n)
                nc.scalar.activation(o_sb[:], o_ps[:], ACT.Copy).then_inc(o_copied, 1)

            for h in range(HG):
                copy_maxima(act, 0, 0, h)
            with act.Fori(0, NIT) as it:
                for j in range(NB):
                    n = it * NB + j
                    for u in range(KT):
                        for h in range(HG):
                            if h == 0:
                                if j > 0 or u > 1:
                                    act.wait_ge(pv_done, n * KT + u - 1)
                                elif u == 1:
                                    act.wait_ge(pv_done, n * KT)
                            exps(n, u, h)
                            if u == 0 and h == 3 and j > 0:
                                copy_result(n - 1)
                        for h in range(HG):
                            if u == COPY_AT[h]:
                                copy_maxima(act, n + 1, (j + 1) % NB, h)
                copy_result(n)

        @block.vector
        def _(dve):
            heads = turn_ps[:].rearrange("p t (h c) -> p t h c", h=HG)

            def divide(n, it, j, s):
                if s == 0:
                    dve.wait_ge(turned, n + 1)
                    nc.vector.reciprocal(inv[:], heads[:, :, :, HD]).then_inc(inv_ready, 1)
                else:
                    dve.wait_ge(inv_ready, n + 1)
                    dst = att[:, ds(it, 1), j // GPB, (j % GPB) * TPG:(j % GPB + 1) * TPG].rearrange("p a t (h c) -> p (a t) h c", h=HG)
                    nc.vector.tensor_tensor(dst, heads[:, :, :, 0:HD], inv[:].unsqueeze(3).broadcast_to([P, TPG, HG, HD]),
                                            ALU.mult).then_inc(att_done, 1)

            nc.vector.memset(o_ps[:], 0.0).then_inc(o_zeroed, 1)
            for k in range(MAXI):
                max_take(dve, 0, 0, k)
            for k in range(2 * LEAD):
                max_take(dve, 1, 1, k)
                row_maxima(dve, 0, 0, k)
            with dve.Fori(0, NIT) as it:
                for j in range(NB):
                    n = it * NB + j
                    for u in range(KT):
                        for i in range(2):
                            k = 2 * (u + LEAD) + i
                            ahead = 1 + k // MAXI
                            max_take(dve, n + ahead, (j + ahead) % NB, k % MAXI)
                            if KT - LEAD <= u < KT - LEAD + 3:
                                row_maxima(dve, n + 1, (j + 1) % NB, 2 * (u - (KT - LEAD)) + i)
                            if u == 3 and j > 0:
                                divide(n - 1, it, j - 1, i)
                for i in range(2):
                    divide(n, it, NB - 1, i)
            dve.wait_ge(att_done, NIT * NB)


def wo_buffers(ctx, nc, tag, aT_ps=None, y_ps=None):
    sb, pb, sem = allocators(ctx, nc, tag)
    return named(
        a=sb("wo_a", [P, TPG, D]), aT=sb("wo_aT", [P, KH, G]), y=sb("wo_y", [P, TPG, D]), w=sb("wo_w", [P, KH, D]),
        aT_ps=pb("wo_aT_ps", [P, KH, G]) if aT_ps is None else aT_ps,
        y_ps=pb("wo_y_ps", [P, TPG, D]) if y_ps is None else y_ps,
        w_loaded=sem("wo_w_loaded"), a_ready=sem("wo_a_ready"), a_turned=sem("wo_a_turned"),
        aT_copied=sem("wo_aT_copied"), y_ready=sem("wo_y_ready"), y_scaled=sem("wo_y_scaled"), x_added=sem("wo_x_added"))


def wo_turn(nc, pe, m, wo, n, a_count):
    pe.wait_ge(wo.a_ready, a_count)
    pe.wait_ge(wo.aT_copied, n * KH)
    for t in range(TPG):
        for half in range(KH):
            last = nc.tensor.transpose(wo.aT_ps[:, half, t * P:(t + 1) * P], wo.a[:, t, half * P:(half + 1) * P], m.ident[:])
    last.then_inc(wo.a_turned, 1)


def wo_project(nc, pe, wo, n):
    pe.wait_ge(wo.aT_copied, n * KH + KH)
    pe.wait_ge(wo.y_scaled, n * 2)
    for t in range(TPG):
        for kh in range(KH):
            last = nc.tensor.matmul(wo.y_ps[:, t], wo.aT[:, kh, t * P:(t + 1) * P], wo.w[:, kh],
                                    start=(kh == 0), stop=(kh == KH - 1))
        if t % 2:
            last.then_inc(wo.y_ready, 1)


def wo_scalar(nc, act, wo, n):
    act.wait_ge(wo.a_turned, n + 1)
    act.wait_ge(wo.y_ready, n * 2)
    for half in range(KH):
        nc.scalar.activation(wo.aT[:, half], wo.aT_ps[:, half], ACT.Copy).then_inc(wo.aT_copied, 1)


def wo_vector(nc, dve, m, wo, n, b, layer):
    for pair in range(2):
        dve.wait_ge(wo.y_ready, n * 2 + pair + 1)
        gate = m.gates[:, layer, 0, ds(b, 1)].broadcast_to([P, 2, D])
        nc.vector.tensor_tensor(wo.y[:, 2 * pair:2 * pair + 2], wo.y_ps[:, 2 * pair:2 * pair + 2], gate, ALU.mult).then_inc(wo.y_scaled, 1)
    for pair in range(2):
        dve.wait_ge(wo.y_scaled, n * 2 + pair + 1)
        xs = m.x[:, ds(n * TPG + 2 * pair, 2)]
        nc.vector.tensor_tensor(xs, xs, wo.y[:, 2 * pair:2 * pair + 2], ALU.add).then_inc(wo.x_added, 1)
    dve.wait_ge(wo.x_added, n * 2 + 2)


ROUTE_STEPS = 2 + 1 + 1 + 1 + TPG + TPG + 1 + 2


def route_buffers(ctx, nc, tag, E):
    sb, pb, sem = allocators(ctx, nc, tag)
    return named(
        E=E, logits=sb("rt_logits", [P, TPG, E]), mx=sb("rt_mx", [P, TPG]), e=sb("rt_e", [P, TPG, E]),
        tot=sb("rt_tot", [P, TPG]), p=sb("rt_p", [P, TPG, E]), top=sb("rt_top", [P, TPG, 8]),
        idx=sb("rt_idx", [P, TPG, 8], U32), idx_f=sb("rt_idx_f", [P, TPG, 2]), hot=sb("rt_hot", [P, 2, TPG, E]),
        logits_ready=sem("rt_logits_ready"), shifted=sem("rt_shifted"), exp_ready=sem("rt_exp_ready"), step=sem("rt_step"))


def route_scalar(nc, act, rt, n):
    act.wait_ge(rt.shifted, n + 1)
    nc.scalar.activation(rt.e[:], rt.logits[:], ACT.Exp).then_inc(rt.exp_ready, 1)


def route_vector(nc, dve, m, rt, n, logits_ps, bias=None):
    E = rt.E
    done = [0]

    def step(ins):
        ins.then_inc(rt.step, 1)
        done[0] += 1

    def steps_done():
        dve.wait_ge(rt.step, n * ROUTE_STEPS + done[0])

    wide = lambda a: a.unsqueeze(2).broadcast_to([P, TPG, E])
    dve.wait_ge(rt.logits_ready, n + 1)
    if bias is None:
        step(nc.vector.tensor_copy(rt.p[:], logits_ps))
    else:
        step(nc.vector.tensor_tensor(rt.p[:], logits_ps, bias.unsqueeze(1).broadcast_to([P, TPG, E]), ALU.add))
    steps_done()
    step(nc.vector.reduce_max(rt.mx[:], rt.p[:], AX.X))
    steps_done()
    nc.vector.tensor_tensor(rt.logits[:], rt.p[:], wide(rt.mx[:]), ALU.subtract).then_inc(rt.shifted, 1)
    dve.wait_ge(rt.exp_ready, n + 1)
    step(nc.vector.reduce_sum(rt.tot[:], rt.e[:], AX.X))
    steps_done()
    step(nc.vector.reciprocal(rt.tot[:], rt.tot[:]))
    steps_done()
    step(nc.vector.tensor_tensor(rt.p[:], rt.e[:], wide(rt.tot[:]), ALU.mult))
    steps_done()
    settle(dve, m)
    for t in range(TPG):
        step(nc.vector.max(rt.top[:, t], rt.p[:, t]))
    steps_done()
    settle(dve, m)
    for t in range(TPG):
        step(nc.vector.max_index(rt.idx[:, t], rt.top[:, t], rt.p[:, t]))
    steps_done()
    step(nc.vector.tensor_copy(rt.idx_f[:], rt.idx[:, :, 0:2]))
    steps_done()
    for k in range(2):
        step(nc.vector.tensor_tensor(rt.hot[:, k], wide(rt.idx_f[:, :, k]),
                                     m.iota[:, 0:E].unsqueeze(1).broadcast_to([P, TPG, E]), ALU.is_equal))
    steps_done()
    assert done[0] == ROUTE_STEPS


def finish_attention0_and_route(nc, m, io):
    with ExitStack() as ctx:
        sb, pb, sem = allocators(ctx, nc, "post0")
        ln, wo, rt = ln_buffers(ctx, nc, "post0"), wo_buffers(ctx, nc, "post0"), route_buffers(ctx, nc, "post0", E0)
        w_router = sb("w_router", [P, KH, E0])
        logits_ps = pb("logits_ps", [P, TPG, E0])
        loaded, z_kept, routed = sem("loaded"), sem("z_kept"), sem("routed")
        att = m.att
        block = ctx.enter_context(nc.Block())

        @block.sync
        def _(sync):
            sync.dma_start(wo.w[:], io.l0_wo).then_inc(wo.w_loaded, 16)
            sync.dma_start(w_router[:], io.w_router).then_inc(loaded, 16)

        LAST = B * GPB - 1

        @block.tensor
        def _(pe):
            def project(n):
                wo_turn(nc, pe, m, wo, n, n + 1)
                wo_project(nc, pe, wo, n)

            def route(n):
                pe.wait_ge(ln.h_ready, n * KH + KH)
                if not isinstance(n, int):
                    pe.wait_ge(rt.step, n * ROUTE_STEPS)
                for t in range(TPG):
                    for kh in range(KH):
                        last = nc.tensor.matmul(logits_ps[:, t], ln.hT[:, kh, t * P:(t + 1) * P], w_router[:, kh],
                                                start=(kh == 0), stop=(kh == KH - 1))
                last.then_inc(rt.logits_ready, 1)

            pe.wait_ge(wo.w_loaded, 16)
            pe.wait_ge(loaded, 16)
            project(0)
            with pe.Fori(0, LAST) as n:
                ln_tensor(nc, pe, m, ln, n)
                project(n + 1)
                route(n)
            ln_tensor(nc, pe, m, ln, LAST)
            pe.wait_ge(rt.step, LAST * ROUTE_STEPS)
            route(LAST)

        @block.scalar
        def _(act):
            def copy_attention(n):
                b, q = n // GPB, n % GPB
                act.wait_ge(wo.a_turned, n)
                src = att[:, ds(b, 1), :, ds(q * TPG, TPG)].rearrange("p a g t c -> p (a g) t c")
                nc.scalar.activation(wo.a[:].rearrange("p t (g c) -> p g t c", g=NHG), src, ACT.Copy).then_inc(wo.a_ready, 1)

            def shift_and_keep(n):
                ln_shift(nc, act, m, ln, n, n // GPB, 0, 1, lambda: act.wait_ge(rt.logits_ready, n))
                act.wait_ge(ln.z_ready, n * TPG + TPG)
                nc.scalar.activation(m.z_all[:, ds(n * TPG, TPG)], ln.z[:], ACT.Copy).then_inc(z_kept, 1)

            copy_attention(0)
            wo_scalar(nc, act, wo, 0)
            ln_root(nc, act, m, ln, 0)
            with act.Fori(0, LAST) as n:
                copy_attention(n + 1)
                shift_and_keep(n)
                wo_scalar(nc, act, wo, n + 1)
                ln_root(nc, act, m, ln, n + 1)
                route_scalar(nc, act, rt, n)
            shift_and_keep(LAST)
            route_scalar(nc, act, rt, LAST)

        @block.vector
        def _(dve):
            def route(n):
                b, q = n // GPB, n % GPB
                route_vector(nc, dve, m, rt, n, logits_ps[:])
                nc.vector.tensor_copy(m.top_p[:, ds(b, 1), :, ds(q * TPG, TPG)].rearrange("p a k t -> p (a k) t"),
                                      rt.top[:, :, 0:2].rearrange("p t k -> p k t")).then_inc(routed, 1)
                nc.vector.tensor_copy(m.top_e[:, ds(b, 1), :, ds(q * TPG, TPG)].rearrange("p a k t -> p (a k) t"),
                                      rt.idx_f[:].rearrange("p t k -> p k t")).then_inc(routed, 1)
                nc.vector.tensor_copy(m.chosen[:, ds(b, 1), :, ds(q * TPG, TPG)].rearrange("p a k t e -> p (a k) (t e)"),
                                      rt.hot[:].rearrange("p k t e -> p k (t e)")).then_inc(routed, 1)
                dve.wait_ge(routed, n * 3 + 3)

            wo_vector(nc, dve, m, wo, 0, 0, 0)
            ln_stats(nc, dve, m, ln, 0, 0)
            with dve.Fori(0, LAST) as n:
                ln_normalize(nc, dve, m, ln, n, n * TPG, lambda: dve.wait_ge(z_kept, n))
                wo_vector(nc, dve, m, wo, n + 1, (n + 1) // GPB, 0)
                ln_stats(nc, dve, m, ln, n + 1, (n + 1) * TPG)
                route(n)
            ln_normalize(nc, dve, m, ln, LAST, LAST * TPG, lambda: dve.wait_ge(z_kept, LAST))
            route(LAST)


def layer0_experts(nc, m, io):
    dispatch(nc, m, io)
    run_experts(nc, m, io)


def dispatch(nc, m, io):
    with ExitStack() as ctx:
        sb, pb, sem = allocators(ctx, nc, "disp")
        S = 2 * TPB
        put_at = sb("put_at", [P, B, 2, TPB], I32)
        get_at = m.get_at
        ones = sb("ones", [P, P], BF16)
        before = [sb(f"before{i}", [P, B, S, E0]) for i in range(2)]
        place = sb("place", [P, B, S, E0])
        pos = sb("pos", [P, B, S])
        base = sb("base", [P, B, S])
        over = sb("over", [P, B, S])
        spot = sb("spot", [P, 2, B, S])
        upto_ps = pb("upto_ps", [P, B, S, E0])
        tile_ps = pb("tile_ps", [P, B, S, E0])
        ones_set, counted, step, put_ready, rows_put = sem("ones_set"), sem("counted"), sem("step"), sem("put_ready"), sem("rows_put")
        block = ctx.enter_context(nc.Block())

        @block.tensor
        def _(pe):
            pe.wait_ge(ones_set, 1)
            for b in range(B):
                hot = m.chosen[:, b].rearrange("p k t e -> p (k t e)")
                nc.tensor.matmul(upto_ps[:, b].rearrange("p s e -> p (s e)"), m.triu_b[:], hot, start=True, stop=True)
                nc.tensor.matmul(tile_ps[:, b].rearrange("p s e -> p (s e)"), ones[:], hot, start=True, stop=True).then_inc(counted, 1)

        @block.vector
        def _(dve):
            n = [0]

            def step_done(*instructions):
                for ins in instructions:
                    ins.then_inc(step, 1)
                    n[0] += 1
                dve.wait_ge(step, n[0])

            nc.vector.memset(ones[:], 1.0).then_inc(ones_set, 1)
            dve.wait_ge(counted, B)
            step_done(nc.vector.memset(before[0][:, :, 0], 0.0),
                      nc.vector.tensor_copy(before[0][:, :, 1:S], tile_ps[:, :, 0:S - 1]))
            src, d = 0, 1
            while d < S:
                a, c = before[src], before[1 - src]
                step_done(nc.vector.tensor_tensor(c[:, :, d:S], a[:, :, d:S], a[:, :, 0:S - d], ALU.add),
                          nc.vector.tensor_copy(c[:, :, 0:d], a[:, :, 0:d]))
                src, d = 1 - src, 2 * d
            hot = m.chosen[:].rearrange("p b k t e -> p b (k t) e")
            step_done(nc.vector.tensor_tensor(place[:], upto_ps[:], before[src][:], ALU.add))
            step_done(nc.vector.tensor_tensor(place[:], place[:], hot, ALU.mult))
            step_done(nc.vector.reduce_sum(pos[:], place[:], AX.X))
            e = m.top_e[:].rearrange("p b k t -> p b (k t)")
            step_done(*[nc.vector.tensor_scalar(base[:, b], e[:, b], float(B * CAP), float(b * CAP - 1), ALU.mult, ALU.add)
                        for b in range(B)],
                      nc.vector.tensor_scalar(over[:], pos[:], float(CAP), float(2 * SLOTS), ALU.is_gt, ALU.mult))
            step_done(nc.vector.tensor_tensor(over[:], over[:], base[:], ALU.add),
                      nc.vector.tensor_scalar(spot[:, 1], pos[:], float(CAP), None, ALU.min))
            step_done(nc.vector.tensor_tensor(spot[:, 0], over[:], pos[:], ALU.add),
                      nc.vector.tensor_tensor(spot[:, 1], spot[:, 1], base[:], ALU.add))
            nc.vector.tensor_copy(put_at[:].rearrange("p b k t -> p b (k t)"), spot[:, 0]).then_inc(put_ready, 1)
            nc.vector.tensor_copy(get_at[:].rearrange("p b k t -> p b (k t)"), spot[:, 1]).then_inc(put_ready, 1)
            dve.wait_ge(put_ready, 2)

        @block.gpsimd
        def _(pool):
            pool.wait_ge(put_ready, 2)
            for b in range(B):
                for k in range(2):
                    for t in range(TPB):
                        nc.gpsimd.indirect_dma_start(
                            out=io.slot_rows, out_offset=bass.IndirectOffsetOnAxis(ap=put_at[:, b, k, t:t + 1], axis=0),
                            in_=m.z_all[:, b * TPB + t], in_offset=None,
                            bounds_check=SLOTS - 1, oob_is_err=False).then_inc(rows_put, 16)
            pool.wait_ge(rows_put, 16 * B * 2 * TPB)


def run_experts(nc, m, io):
    with ExitStack() as ctx:
        sb, pb, sem = allocators(ctx, nc, "moe")
        ET = B * CAP // P
        NSL = B * CAP
        rows = sb("rows", [P, 2, ET, D])
        w_gf = sb("w_gf", [P, 2, KH, 2 * HID])
        w_pr = sb("w_pr", [P, 2, D])
        hT = sb("hT", [P, KH, NSL])
        act_gate = sb("act_gate", [P, NSL])
        hid = sb("hid", [P, NSL])
        y = sb("y", [P, 2, ET, D])
        rT_ps, gf_ps, y_ps = pb("rT_ps", [P, KH, NSL]), pb("gf_ps", [P, 2, NSL]), pb("y_ps", [P, ET, D])
        loaded = [sem(f"loaded{r}") for r in range(2)]
        stored = [sem(f"stored{r}") for r in range(2)]
        turned, h_ready, gf_ready, silu_ready, hid_ready = sem("turned"), sem("h_ready"), sem("gf_ready"), sem("silu_ready"), sem("hid_ready")
        y_ready, y_scaled = sem("y_ready"), sem("y_scaled")
        block = ctx.enter_context(nc.Block())
        tiles = lambda dram: dram.rearrange("(e t p) d -> e p t d", e=E0, p=P)

        @block.sync
        def _(sync):
            def load(e, r):
                sync.dma_start(rows[:, r], tiles(io.slot_rows)[ds(e, 1)].rearrange("a p t d -> (a p) t d")).then_inc(loaded[r], 16)
                sync.dma_start(w_gf[:, r], io.w_gate_fc[ds(e, 1)].rearrange("a p k n -> (a p) k n")).then_inc(loaded[r], 16)
                sync.dma_start(w_pr[:, r], io.w_proj[ds(e, 1)].rearrange("a p n -> (a p) n")).then_inc(loaded[r], 16)

            for r in range(2):
                load(r, r)
            with sync.Fori(0, E0 // 2 - 1) as i:
                for r in range(2):
                    sync.wait_ge(y_ready, (i * 2 + r + 1) * 2)
                    load(i * 2 + r + 2, r)

        @block.gpsimd
        def _(pool):
            with pool.Fori(0, E0 // 2) as i:
                for r in range(2):
                    e = i * 2 + r
                    pool.wait_ge(y_scaled, e * 2 + 2)
                    pool.dma_start(tiles(io.slot_out)[ds(e, 1)].rearrange("a p t d -> (a p) t d"), y[:, r]).then_inc(stored[r], 16)
            for r in range(2):
                pool.wait_ge(stored[r], 16 * (E0 // 2))

        @block.tensor
        def _(pe):
            def turn(e, i, r):
                pe.wait_ge(loaded[r], 48 * (i + 1))
                pe.wait_ge(h_ready, e * 2 * KH)
                for t in range(ET):
                    for half in range(KH):
                        last = nc.tensor.transpose(rT_ps[:, half, t * P:(t + 1) * P], rows[:, r, t, half * P:(half + 1) * P], m.ident[:])
                last.then_inc(turned, 1)

            def expert(i, r, last_one=False):
                e = i * 2 + r
                pe.wait_ge(h_ready, (e + 1) * 2 * KH)
                pe.wait_ge(hid_ready, e)
                for v in range(2):
                    for kh in range(KH):
                        last = nc.tensor.matmul(gf_ps[:, v], w_gf[:, r, kh, v * HID:(v + 1) * HID], hT[:, kh],
                                                start=(kh == 0), stop=(kh == KH - 1))
                    last.then_inc(gf_ready, 1)
                if not last_one:
                    turn(e + 1, i + r, 1 - r)
                pe.wait_ge(hid_ready, e + 1)
                pe.wait_ge(y_scaled, e * 2)
                for t in range(ET):
                    last = nc.tensor.matmul(y_ps[:, t], hid[:, t * P:(t + 1) * P], w_pr[:, r], start=True, stop=True)
                    if t % 2:
                        last.then_inc(y_ready, 1)

            turn(0, 0, 0)
            with pe.Fori(0, E0 // 2 - 1) as i:
                for r in range(2):
                    expert(i, r)
            expert(E0 // 2 - 1, 0)
            expert(E0 // 2 - 1, 1, last_one=True)

        @block.scalar
        def _(act):
            def shift(e):
                act.wait_ge(turned, e + 1)
                act.wait_ge(gf_ready, e * 2)
                for half in range(KH):
                    for b in range(B):
                        cols = slice(b * CAP, (b + 1) * CAP)
                        nc.scalar.activation(hT[:, half, cols], rT_ps[:, half, cols], ACT.Identity,
                                             bias=m.modv[:, 0, 2, half, b:b + 1],
                                             scale=m.modv[:, 0, 3, half, b:b + 1]).then_inc(h_ready, 1)

            def silu(e):
                act.wait_ge(gf_ready, e * 2 + 1)
                act.wait_ge(hid_ready, e)
                nc.scalar.activation(act_gate[:], gf_ps[:, 0], ACT.Silu).then_inc(silu_ready, 1)

            shift(0)
            with act.Fori(0, E0 - 1) as e:
                silu(e)
                shift(e + 1)
            silu(E0 - 1)

        @block.vector
        def _(dve):
            with dve.Fori(0, E0 // 2) as i:
                for r in range(2):
                    e = i * 2 + r
                    dve.wait_ge(silu_ready, e + 1)
                    dve.wait_ge(gf_ready, e * 2 + 2)
                    dve.wait_ge(y_ready, e * 2)
                    nc.vector.tensor_tensor(hid[:], act_gate[:], gf_ps[:, 1], ALU.mult).then_inc(hid_ready, 1)
                    dve.wait_ge(stored[r], i * 16)
                    for b in range(B):
                        dve.wait_ge(y_ready, e * 2 + b + 1)
                        gate = m.gates[:, 0, 1, b].unsqueeze(1).broadcast_to([P, 2, D])
                        nc.vector.tensor_tensor(y[:, r, 2 * b:2 * b + 2], y_ps[:, 2 * b:2 * b + 2], gate, ALU.mult).then_inc(y_scaled, 1)


def linear_attention(nc, m, io):
    with ExitStack() as ctx:
        sb, pb, sem = allocators(ctx, nc, "lin")
        ln = ln_buffers(ctx, nc, "lin")
        HV = NHH * AUG
        HW = P // HG
        qk_ps = pb("qk_ps", [P, 4, G])
        kv_ps = pb("kv_ps", [P, 2 * D])
        o_ps = pb("o_ps", [P, NHG, P])
        st_ps = ln.zT[:, 0, 0:NH * AUG]
        turn_ps = ln.zT[:, 1].rearrange("p (g n) -> p g n", n=P)
        wo = wo_buffers(ctx, nc, "lin", qk_ps[:, 0:2], ln.zT[:].rearrange("p a n -> p (a n)").rearrange("p (t d) -> p t d", d=D))
        w_qk, w_kv = sb("w_qk", [P, KH, 2 * D]), sb("w_kv", [P, KH, 2 * D])
        head_of = sb("head_of", [P, NHH])
        qkT = sb("qkT", [P, 4, G])
        q_wide = sb("q_wide", [P, 2, 2, NHH, P])
        masked = sb("masked", [P, 2, NHH, P])
        k_tok = sb("k_tok", [P, 2, D])
        va = sb("va", [P, 2, NH * AUG])
        kv_new = sb("kv_new", [P, 2, HV])
        kv_state = sb("kv_state", [P, 2, NHH, HW])
        o_sb = sb("o_sb", [P, NHG, P])
        den = sb("den", [P, NH])
        got = sb("got", [P, TPG, 2, D])
        rows_in = [sem(f"rows_in{t}") for t in range(TPG)]
        row_added = sem("row_added")
        loaded, ones_set = sem("loaded"), sem("ones_set")
        qk_ready, qk_copied = sem("qk_ready"), sem("qk_copied")
        wide_ready = (sem("wide_ready0"), sem("wide_ready1"))
        kv_ready, k_copied, v_copied = sem("kv_ready"), sem("k_copied"), sem("v_copied")
        o_copied, o_turned = sem("o_copied"), sem("o_turned")
        s_ready, masked_ready, o_ready = sem("s_ready"), sem("masked_ready"), sem("o_ready")
        st_ready, st_masked, st_added, den_step = sem("st_ready"), sem("st_masked"), sem("st_added"), sem("den_step")
        block = ctx.enter_context(nc.Block())
        TB1 = TPB + 1

        @block.sync
        def _(sync):
            sync.dma_start(w_qk[:], io.l1_wqk).then_inc(loaded, 16)
            sync.dma_start(w_kv[:], io.l1_wkv).then_inc(loaded, 16)
            sync.dma_start(head_of[:], io.head_of).then_inc(loaded, 16)
            sync.dma_start(wo.w[:], io.l1_wo).then_inc(loaded, 16)

        @block.gpsimd
        def _(pool):
            nc.gpsimd.memset(va[:].rearrange("p r (h c) -> p (r h) c", c=AUG)[:, :, HD:AUG], 1.0).then_inc(ones_set, 1)
            for tile in range(NT):
                t = tile % TPG
                if t == 0 and tile > 0:
                    pool.wait_ge(row_added, 2 * tile)
                for k in range(2):
                    nc.gpsimd.indirect_dma_start(
                        out=got[:, t, k], out_offset=None, in_=io.slot_out,
                        in_offset=bass.IndirectOffsetOnAxis(ap=m.get_at[:, tile // TPB, k, tile % TPB:tile % TPB + 1], axis=0),
                        bounds_check=SLOTS - 1, oob_is_err=False).then_inc(rows_in[t], 16)

        Q_HALVES, K_HALVES = (0, 1), (2, 3)

        @block.tensor
        def _(pe):
            def tokens_kv(n, t):
                c = n * TPG + t
                pe.wait_ge(k_copied, c)
                pe.wait_ge(v_copied, c)
                for kh in range(KH):
                    last = nc.tensor.matmul(kv_ps[:], ln.hT[:, kh, t * P:(t + 1) * P], w_kv[:, kh],
                                            start=(kh == 0), stop=(kh == KH - 1))
                last.then_inc(kv_ready, 1)

            def turn_sums(c):
                pe.wait_ge(o_copied, c + 1)
                pe.wait_ge(wo.a_ready, c)
                for g in range(NHG):
                    last = nc.tensor.transpose(turn_ps[:, g], o_sb[:, g], m.ident[:])
                last.then_inc(o_turned, 1)

            def project(halves):
                for a in halves:
                    for kh in range(KH):
                        last = nc.tensor.matmul(qk_ps[:, a], w_qk[:, kh, a * P:(a + 1) * P], ln.hT[:, kh],
                                                start=(kh == 0), stop=(kh == KH - 1))
                    last.then_inc(qk_ready, 1)

            ln_tensor(nc, pe, m, ln, 0)
            pe.wait_ge(loaded, 64)
            pe.wait_ge(ones_set, 1)
            pe.wait_ge(ln.h_ready, KH)
            project(K_HALVES)
            with pe.Fori(0, B) as b:
                with pe.Fori(0, GPB) as q:
                    n = group_of(b, q)
                    pe.wait_ge(wo.aT_copied, n * KH)
                    project(Q_HALVES)
                    tokens_kv(n, 0)
                    for t in range(TPG):
                        c = n * TPG + t
                        tok = slice(t * P, (t + 1) * P)
                        if t == 0:
                            pe.wait_ge(qk_copied, n * 4 + 4)
                        for half in range(2):
                            pe.wait_ge(wide_ready[half], c + 1)
                            for g in range(2):
                                last = nc.tensor.matmul(qk_ps[:, 2 * half + g], qkT[:, 2 + half, tok],
                                                        q_wide[:, t % 2, half, g * HG:(g + 1) * HG].rearrange("p h n -> p (h n)"),
                                                        start=True, stop=True)
                            last.then_inc(s_ready, 1)
                        if t + 1 < TPG:
                            tokens_kv(n, t + 1)
                        if t > 0:
                            turn_sums(c - 1)
                        pe.wait_ge(o_copied, c)
                        pe.wait_ge(st_added, b * TB1 + q * TPG + t + 1)
                        pe.wait_ge(v_copied, c + 1)
                        for g in range(NHG):
                            half, h0 = g // 2, g % 2 * HG
                            nc.tensor.matmul(o_ps[:, g], kv_state[:, half, h0:h0 + HG].rearrange("p h c -> p (h c)"),
                                             qkT[:, half, tok], start=True, stop=False, skip_group_check=True)
                            if g % 2 == 0:
                                pe.wait_ge(masked_ready, c * 2 + half + 1)
                            for h in range(HG):
                                hh = g * HG + h
                                last = nc.tensor.matmul(o_ps[HW * h:HW * h + AUG, g], va[:, t % 2, hh * AUG:(hh + 1) * AUG],
                                                        masked[:, half, h0 + h], start=False, stop=True, skip_group_check=True)
                        last.then_inc(o_ready, 1)
                        pe.wait_ge(k_copied, c + 1)
                        if t == 0:
                            pe.wait_ge(wo.y_scaled, n * 2)
                        for half in range(2):
                            last = nc.tensor.matmul(st_ps[:, half * HV:(half + 1) * HV], k_tok[:, t % 2, half * HALF:(half + 1) * HALF],
                                                    va[:, t % 2, half * HV:(half + 1) * HV], start=True, stop=True)
                        last.then_inc(st_ready, 1)
                    turn_sums(n * TPG + TPG - 1)
                    pe.wait_ge(ln.z_ready, (n + 2) * TPG)
                    for half in range(KH):
                        if half == 0:
                            pe.wait_ge(st_added, b * TB1 + q * TPG + TPG + 1)
                        else:
                            pe.wait_ge(wo.a_ready, (n + 1) * TPG)
                        for t in range(TPG):
                            last = nc.tensor.transpose(ln.zT[:, half, t * P:(t + 1) * P], ln.z[:, t, half * P:(half + 1) * P], m.ident[:])
                    last.then_inc(ln.zT_ready, 1)
                    wo_turn(nc, pe, m, wo, n, n * TPG + TPG)
                    pe.wait_ge(ln.h_ready, (n + 2) * KH)
                    project(K_HALVES)
                    wo_project(nc, pe, wo, n)

        @block.scalar
        def _(act):
            def widen(t):
                for h in range(NHH):
                    ins = nc.scalar.activation(q_wide[:, t % 2, 1, h], qkT[:, 1, t * P:(t + 1) * P], ACT.Copy, scale=head_of[:, h:h + 1])
                ins.then_inc(wide_ready[1], 1)

            def copy_sums(c):
                act.wait_ge(o_ready, c + 1)
                act.wait_ge(o_turned, c)
                nc.scalar.activation(o_sb[:], o_ps[:], ACT.Copy).then_inc(o_copied, 1)

            act.wait_ge(ones_set, 1)
            act.wait_ge(loaded, 64)
            ln_root(nc, act, m, ln, 0)
            ln_shift(nc, act, m, ln, 0, 0, 1, 0)
            with act.Fori(0, B) as b:
                with act.Fori(0, GPB) as q:
                    n = group_of(b, q)
                    b_next, _ = next_group(b, q)
                    act.wait_ge(qk_copied, n * 4 + 4)
                    widen(0)
                    for t in range(TPG):
                        c = n * TPG + t
                        act.wait_ge(kv_ready, c + 1)
                        nc.scalar.activation(va[:, t % 2].rearrange("p (h c) -> p h c", c=AUG)[:, :, 0:HD],
                                             kv_ps[:, D:2 * D].rearrange("p (h c) -> p h c", c=HD), ACT.Copy).then_inc(v_copied, 1)
                        if t > 0:
                            copy_sums(c - 1)
                        if t + 1 < TPG:
                            widen(t + 1)
                    ln_root(nc, act, m, ln, n + 1)
                    copy_sums(n * TPG + TPG - 1)
                    ln_shift(nc, act, m, ln, n + 1, b_next, 1, 0)
                    wo_scalar(nc, act, wo, n)

        @block.vector
        def _(dve):
            def widen(t):
                nc.vector.tensor_tensor(q_wide[:, t % 2, 0],
                                        qkT[:, 0, t * P:(t + 1) * P].unsqueeze(1).broadcast_to([P, NHH, P]),
                                        head_of[:].unsqueeze(2).broadcast_to([P, NHH, P]), ALU.mult).then_inc(wide_ready[0], 1)

            def tokens_k(n, t):
                dve.wait_ge(v_copied, n * TPG + t + 1)
                nc.vector.tensor_scalar(k_tok[:, t % 2], kv_ps[:, 0:D], 0.0, EPS_LIN, ALU.max, ALU.add).then_inc(k_copied, 1)

            def add_rows(n, b, tile, k):
                for t in range(TPG):
                    if k == 0:
                        dve.wait_ge(rows_in[t], 32 * (n + 1))
                    else:
                        dve.wait_ge(row_added, n * 2 * TPG + t + 1)
                    x = m.x[:, ds(tile + t, 1)].rearrange("p a d -> p (a d)")
                    p = m.top_p[:, ds(b, 1), k, ds(tile % TPB + t, 1)].rearrange("p a t -> p (a t)")
                    nc.vector.scalar_tensor_tensor(x, got[:, t, k], p, x, ALU.mult, ALU.add).then_inc(row_added, 1)

            def relu(halves, n, first):
                for i, a in enumerate(halves):
                    dve.wait_ge(qk_ready, n * 4 + first + i + 1)
                    nc.vector.tensor_scalar(qkT[:, a], qk_ps[:, a], 0.0, EPS_LIN, ALU.max, ALU.add).then_inc(qk_copied, 1)

            def divide(n, t):
                c = n * TPG + t
                heads = turn_ps.rearrange("p g (h c) -> p (g h) c", c=HW)
                dve.wait_ge(o_turned, c + 1)
                nc.vector.tensor_scalar(den[:], heads[:, :, HD], EPS_LIN, None, ALU.add).then_inc(den_step, 1)
                dve.wait_ge(den_step, c * 2 + 1)
                nc.vector.reciprocal(den[:], den[:]).then_inc(den_step, 1)
                dve.wait_ge(den_step, c * 2 + 2)
                if t == 0:
                    dve.wait_ge(wo.a_turned, n)
                nc.vector.tensor_tensor(wo.a[:, t].rearrange("p (h c) -> p h c", c=HD), heads[:, :, 0:HD],
                                        den[:].unsqueeze(2).broadcast_to([P, NH, HD]), ALU.mult).then_inc(wo.a_ready, 1)

            def group(b, q, last_one=False):
                n = group_of(b, q)
                b_next, tile = next_group(b, q)
                dve.wait_ge(o_ready, n * TPG)
                relu(Q_HALVES, n, 2)
                dve.wait_ge(qk_copied, n * 4 + 3)
                widen(0)
                tokens_k(n, 0)
                for t in range(TPG):
                    c = n * TPG + t
                    for half in range(2):
                        dve.wait_ge(s_ready, c * 2 + half + 1)
                        nc.vector.tensor_tensor(masked[:, half],
                                                qk_ps[:, 2 * half:2 * half + 2].rearrange("p g (h n) -> p (g h) n", n=P),
                                                m.triu[:].unsqueeze(1).broadcast_to([P, NHH, P]), ALU.mult).then_inc(masked_ready, 1)
                    if t + 1 < TPG:
                        widen(t + 1)
                        tokens_k(n, t + 1)
                    if t == TPG - 1:
                        ln_normalize(nc, dve, m, ln, n + 1, tile, lambda: None)
                    dve.wait_ge(st_ready, c + 1)
                    nc.vector.tensor_tensor(kv_new[:].rearrange("p a (h c) -> p a h c", c=AUG),
                                            st_ps.rearrange("p (a h c) -> p a h c", a=2, c=AUG),
                                            head_of[:].unsqueeze(1).unsqueeze(3).broadcast_to([P, 2, NHH, AUG]),
                                            ALU.mult).then_inc(st_masked, 1)
                    dve.wait_ge(st_masked, c + 1)
                    dve.wait_ge(o_ready, c + 1)
                    state = kv_state[:, :, :, 0:AUG]
                    nc.vector.tensor_tensor(state, state, kv_new[:].rearrange("p a (h c) -> p a h c", c=AUG), ALU.add).then_inc(st_added, 1)
                    if t > 0:
                        divide(n, t - 1)
                    if t < 2 and not last_one:
                        add_rows(n + 1, b_next, tile, t)
                    if t == 2:
                        if not last_one:
                            dve.wait_ge(row_added, (n + 2) * 2 * TPG)
                        ln_stats(nc, dve, m, ln, n + 1, tile)
                divide(n, TPG - 1)
                relu(K_HALVES, n + 1, 0)
                wo_vector(nc, dve, m, wo, n, b, 1)

            for k in range(2):
                add_rows(0, 0, 0, k)
            dve.wait_ge(row_added, 2 * TPG)
            ln_stats(nc, dve, m, ln, 0, 0)
            ln_normalize(nc, dve, m, ln, 0, 0, lambda: None)
            dve.wait_ge(loaded, 64)
            relu(K_HALVES, 0, 0)
            for b in range(B):
                if b:
                    dve.wait_ge(o_ready, b * TPB)
                nc.vector.memset(kv_state[:], 0.0).then_inc(st_added, 1)
                with dve.Fori(0, GPB - (b == B - 1)) as q:
                    group(b, q)
            group(B - 1, GPB - 1, last_one=True)


def project_layer1_ffn(nc, m, io):
    with ExitStack() as ctx:
        sb, pb, sem = allocators(ctx, nc, "ffn1")
        ln, sp, rt = ln_buffers(ctx, nc, "ffn1", ring=2), split_buffers(ctx, nc, "ffn1"), route_buffers(ctx, nc, "ffn1", E1)
        w_qkv, b_qk, b_v = sb("w_qkv", [P, KH, 3 * D]), sb("b_qk", [P, 4]), sb("b_v", [P, D])
        w_gate, b_gate = sb("w_gate", [P, KH, E1]), sb("b_gate", [P, E1])
        w_exp, b_exp = sb("w_exp", [P, KH, E1 * D]), sb("b_exp", [E1, D])
        va = sb("va", [P, TPG, NH * AUG])
        shares = sb("shares", [P, 2, TPG, E1])
        comb = sb("comb", [P, TPG, E1])
        combT = sb("combT", [E1, TPG, P])
        acc = sb("acc", [P, TPG, D])
        acc_g = sb("acc_g", [P, TPG, D])
        qk_ps = pb("qk_ps", [P, 4, G])
        v_ps = pb("v_ps", [P, TPG, D])
        logits_ps = ln.zT[:, 0, 0:TPG * E1].rearrange("p (t e) -> p t e", e=E1)
        combT_ps = ln.zT[0:E1, 1].rearrange("p (t n) -> p t n", n=P)
        loaded, ones_set = sem("loaded"), sem("ones_set")
        qk_ready, v_ready, v_copied, v_stored = sem("qk_ready"), sem("v_ready"), sem("v_copied"), sem("v_stored")
        share_ready, comb_ready, combT_ready, combT_copied = sem("share_ready"), sem("comb_ready"), sem("combT_ready"), sem("combT_copied")
        bias_ready, ex_ready, acc_step, gated, x_added = sem("bias_ready"), sem("ex_ready"), sem("acc_step"), sem("gated"), sem("x_added")
        NACC = E1 + 1
        block = ctx.enter_context(nc.Block())

        @block.sync
        def _(sync):
            for dst, src in ((w_qkv, io.w_qkv), (b_qk, io.b_qk), (b_v, io.b_v), (w_gate, io.w_gate1), (b_gate, io.b_gate1),
                             (w_exp, io.w_exp), (b_exp, io.b_exp)):
                sync.dma_start(dst[:], src).then_inc(loaded, 16)
            with sync.Fori(0, B) as b:
                with sync.Fori(0, GPB) as q:
                    n = group_of(b, q)
                    store_values(sync, io, va, v_copied, v_stored, n, b, q)
                    split_store(sync, io, sp, n, b, q, paired=False)
            sync.wait_ge(v_stored, B * GPB * 16 * NHG)
            sync.wait_ge(sp.stored, B * GPB * 16 * 4 * NPART)

        @block.gpsimd
        def _(pool):
            nc.gpsimd.memset(va[:].rearrange("p t (h c) -> p (t h) c", c=AUG)[:, :, HD:AUG], 1.0).then_inc(ones_set, 1)

        @block.tensor
        def _(pe):
            ln_tensor(nc, pe, m, ln, 0)
            pe.wait_ge(loaded, 7 * 16)
            with pe.Fori(0, B * GPB // 2) as i:
                for slot in range(2):
                    n = 2 * i + slot
                    hT = ln.hT[:, slot * KH:(slot + 1) * KH]
                    pe.wait_ge(ln.h_ready, n * KH + KH)
                    for t in range(TPG):
                        for kh in range(KH):
                            last = nc.tensor.matmul(logits_ps[:, t], hT[:, kh, t * P:(t + 1) * P], w_gate[:, kh],
                                                    start=(kh == 0), stop=(kh == KH - 1))
                    last.then_inc(rt.logits_ready, 1)
                    pe.wait_ge(acc_step, n * TPG * NACC)
                    for a in range(4):
                        for kh in range(KH):
                            last = nc.tensor.matmul(qk_ps[:, a], w_qkv[:, kh, a * P:(a + 1) * P], hT[:, kh],
                                                    start=(kh == 0), stop=(kh == KH - 1))
                        last.then_inc(qk_ready, 1)
                    for t in range(TPG):
                        for kh in range(KH):
                            last = nc.tensor.matmul(v_ps[:, t], hT[:, kh, t * P:(t + 1) * P], w_qkv[:, kh, 2 * D:3 * D],
                                                    start=(kh == 0), stop=(kh == KH - 1))
                        if t % 2:
                            last.then_inc(v_ready, 1)
                    pe.wait_ge(comb_ready, n + 1)
                    for t in range(TPG):
                        last = nc.tensor.transpose(combT_ps[:, t], comb[:, t], m.ident[:])
                    last.then_inc(combT_ready, 1)
                    pe.wait_ge(combT_copied, n + 1)
                    pe.wait_ge(v_copied, n * 2 + 2)
                    for t in range(TPG):
                        last = nc.tensor.matmul(v_ps[:, t], combT[:, t], b_exp[:], start=True, stop=True)
                    last.then_inc(bias_ready, 1)
                    for t in range(TPG):
                        if t == TPG - 1:
                            ln_tensor(nc, pe, m, ln, n + 1)
                        for pair in range(E1 // 2):
                            if t == 0:
                                pe.wait_ge(sp.whole_ready, n * 4 + pair + 1)
                            else:
                                pe.wait_ge(acc_step, (n * TPG + t - 1) * NACC + 1 + 2 * pair + 2)
                            for kh in range(KH):
                                last = nc.tensor.matmul(qk_ps[:, pair], hT[:, kh, t * P:(t + 1) * P],
                                                        w_exp[:, kh, pair * 2 * D:(pair + 1) * 2 * D],
                                                        start=(kh == 0), stop=(kh == KH - 1))
                            last.then_inc(ex_ready, 1)

        @block.scalar
        def _(act):
            act.wait_ge(loaded, 7 * 16)
            act.wait_ge(ones_set, 1)
            ln_root(nc, act, m, ln, 0)
            ln_shift(nc, act, m, ln, 0, 0, 1, 1)
            with act.Fori(0, B) as b:
                with act.Fori(0, GPB) as q:
                    n = group_of(b, q)
                    b_next, _ = next_group(b, q)
                    route_scalar(nc, act, rt, n)
                    act.wait_ge(sp.lo_ready, n * 4)
                    for a in range(4):
                        act.wait_ge(qk_ready, n * 4 + a + 1)
                        nc.scalar.activation(sp.whole[:, a], qk_ps[:, a], ACT.Identity, bias=b_qk[:, a:a + 1]).then_inc(sp.whole_ready, 1)
                    for a in range(4):
                        split_scalar_hi(nc, act, sp, n, a)
                    act.wait_ge(combT_ready, n + 1)
                    act.wait_ge(bias_ready, n)
                    nc.scalar.activation(combT[:], combT_ps, ACT.Copy).then_inc(combT_copied, 1)
                    for a in range(4):
                        split_scalar_mid(nc, act, sp, n, a)
                    ln_root(nc, act, m, ln, n + 1)
                    ln_shift(nc, act, m, ln, n + 1, b_next, 1, 1, lambda: act.wait_ge(ex_ready, n * TPG * (E1 // 2)), (n + 1) % 2)

        @block.vector
        def _(dve):
            ln_stats(nc, dve, m, ln, 0, 0)
            ln_normalize(nc, dve, m, ln, 0, 0, lambda: None)
            dve.wait_ge(loaded, 7 * 16)
            dve.wait_ge(ones_set, 1)
            with dve.Fori(0, B) as b:
                with dve.Fori(0, GPB) as q:
                    n = group_of(b, q)
                    _, tile = next_group(b, q)
                    route_vector(nc, dve, m, rt, n, logits_ps, b_gate[:])
                    for k in range(2):
                        nc.vector.tensor_tensor(shares[:, k], rt.hot[:, k],
                                                rt.top[:, :, k:k + 1].broadcast_to([P, TPG, E1]), ALU.mult).then_inc(share_ready, 1)
                    dve.wait_ge(share_ready, n * 2 + 2)
                    nc.vector.tensor_tensor(comb[:], shares[:, 0], shares[:, 1], ALU.add).then_inc(comb_ready, 1)
                    dve.wait_ge(v_stored, n * (16 * NHG))
                    for pair in range(2):
                        dve.wait_ge(v_ready, n * 2 + pair + 1)
                        for t in (2 * pair, 2 * pair + 1):
                            ins = nc.vector.tensor_tensor(va[:, t].rearrange("p (h c) -> p h c", c=AUG)[:, :, 0:HD],
                                                          v_ps[:, t].rearrange("p (h c) -> p h c", c=HD),
                                                          b_v[:].rearrange("p (h c) -> p h c", c=HD), ALU.add)
                        ins.then_inc(v_copied, 1)
                    for a in range(4):
                        split_vector_rest(nc, dve, sp, n, a)
                    for a in range(4):
                        split_vector_lo(nc, dve, sp, n, a)
                    dve.wait_ge(comb_ready, n + 1)
                    dve.wait_ge(bias_ready, n + 1)
                    for t in range(TPG):
                        if t == 1:
                            ln_stats(nc, dve, m, ln, n + 1, tile)
                        if t == 2:
                            ln_normalize(nc, dve, m, ln, n + 1, tile, lambda: None)
                        s = (n * TPG + t) * NACC
                        nc.vector.tensor_copy(acc[:, t], v_ps[:, t]).then_inc(acc_step, 1)
                        for e in range(E1):
                            if e % 2 == 0:
                                dve.wait_ge(ex_ready, (n * TPG + t) * (E1 // 2) + e // 2 + 1)
                            dve.wait_ge(acc_step, s + 1 + e)
                            nc.vector.scalar_tensor_tensor(acc[:, t], qk_ps[:, e // 2, (e % 2) * D:(e % 2 + 1) * D], comb[:, t, e:e + 1],
                                                           acc[:, t], ALU.mult, ALU.add).then_inc(acc_step, 1)
                    dve.wait_ge(acc_step, (n + 1) * TPG * NACC)
                    gate = m.gates[:, 1, 1, ds(b, 1)].broadcast_to([P, TPG, D])
                    nc.vector.tensor_tensor(acc_g[:], acc[:], gate, ALU.mult).then_inc(gated, 1)
                    dve.wait_ge(gated, n + 1)
                    xs = m.x[:, ds(n * TPG, TPG)]
                    nc.vector.tensor_tensor(xs, xs, acc_g[:], ALU.add).then_inc(x_added, 1)
                    dve.wait_ge(x_added, n + 1)


def add_attention_and_store(nc, m, io):
    with ExitStack() as ctx:
        sb, pb, sem = allocators(ctx, nc, "end")
        scaled = sb("scaled", [P, 2, TPG, D])
        y_scaled, y_added, out_stored = sem("y_scaled"), sem("y_added"), sem("out_stored")
        out = io.out.rearrange("(t p) d -> p t d", p=P)
        block = ctx.enter_context(nc.Block())

        @block.vector
        def _(dve):
            for n in range(B * GPB):
                b, q = n // GPB, n % GPB
                if n >= 2:
                    dve.wait_ge(y_added, n - 1)
                src = m.att[:, b, :, q * TPG:(q + 1) * TPG].rearrange("p g t c -> p t g c")
                for t in range(TPG):
                    ins = nc.vector.tensor_tensor(scaled[:, n % 2, t].rearrange("p (g c) -> p g c", g=NHG), src[:, t],
                                                  m.gates[:, 1, 1, b].rearrange("p (g c) -> p g c", g=NHG), ALU.mult)
                ins.then_inc(y_scaled, 1)
                dve.wait_ge(y_scaled, n + 1)
                xs = m.x[:, n * TPG:(n + 1) * TPG]
                nc.vector.tensor_tensor(xs, xs, scaled[:, n % 2], ALU.add).then_inc(y_added, 1)

        @block.sync
        def _(sync):
            for n in range(B * GPB):
                sync.wait_ge(y_added, n + 1)
                sync.dma_start(out[:, n * TPG:(n + 1) * TPG], m.x[:, n * TPG:(n + 1) * TPG]).then_inc(out_stored, 16)
            sync.wait_ge(out_stored, 16 * B * GPB)


class State:
    pass


def declare_state(nc, ctx):
    sb, _, sem = allocators(ctx, nc, "all")
    m = State()
    m.settled = sem("settled")
    m.x_loaded = [sem(f"x_loaded{b}") for b in range(B)]
    m.x = sb("x_res", [P, NT, D])
    m.ident, m.ident_b = sb("ident", [P, P]), sb("ident_b", [P, P], BF16)
    m.triu, m.triu_b = sb("triu", [P, P]), sb("triu_b", [P, P], BF16)
    m.iota, m.eps = sb("iota", [P, E0]), sb("eps", [P, 1])
    m.modv = sb("modv", [P, 2, 4, KH, B])
    m.gates = sb("gates", [P, 2, 2, B, D])
    m.top_p, m.top_e = sb("top_p", [P, B, 2, TPB]), sb("top_e", [P, B, 2, TPB])
    m.get_at = sb("get_at", [P, B, 2, TPB], I32)
    m.chosen = sb("chosen", [P, B, 2, TPB, E0], BF16)
    return m


def build_program(nc, tensors, out):
    dram = lambda name, shape, dt=F32: nc.dram_tensor(name, shape, dt).ap()
    io = named(out=out, **tensors,
               q_parts=dram("q_parts", [NPART, B, NHG, HG, HD, T], BF16),
               k_parts=dram("k_parts", [NPART, B, NHG, HG, HD, T], BF16),
               v_rows=dram("v_rows", [B, NHG, P, TPB, VROW]),
               slot_rows=dram("slot_rows", [SLOTS, D]), slot_out=dram("slot_out", [SLOTS, D]))
    with ExitStack() as ctx:
        m = declare_state(nc, ctx)
        load_and_modulate(nc, m, io)
        project_layer0(nc, m, io)
        with nc.sbuf_tensor("z_all", [P, NT, D], F32) as z_all:
            m.z_all = z_all
            with nc.sbuf_tensor("att0", [P, B, NHG, TPB, HG * HD], F32) as att:
                m.att = att
                softmax_attention(nc, m, io, "att_l0", zero_slots=True)
                finish_attention0_and_route(nc, m, io)
            layer0_experts(nc, m, io)
        linear_attention(nc, m, io)
        project_layer1_ffn(nc, m, io)
        with nc.sbuf_tensor("att1", [P, B, NHG, TPB, HG * HD], F32) as att:
            m.att = att
            softmax_attention(nc, m, io, "att_l1")
            add_attention_and_store(nc, m, io)


def host_layout(inputs):
    f = lambda name: np.ascontiguousarray(inputs[name])
    halves = lambda w: np.ascontiguousarray(w.reshape(KH, P, -1).transpose(1, 0, 2))
    pairs = lambda w: w.reshape(NH, HD // 2, 2, D).transpose(2, 0, 1, 3).reshape(D, D)
    pos = np.arange(T, dtype=np.float32)[None, :]
    freq = np.exp(np.float32(-np.log(10000.0)) * np.arange(0, HD, 2, dtype=np.float32) / np.float32(HD)).astype(np.float32)
    angle = np.tile(freq, NH)[:, None] * pos
    pi = np.arange(P)
    out = {
        "x": f("L0_attn_x").reshape(B * T, D),
        "c_t": np.stack([f("L0_c").T.reshape(KH, P, B), f("L1_c").T.reshape(KH, P, B)]).transpose(2, 0, 1, 3),
        "wmod": np.stack([halves(f("L0_wmod")), halves(f("L1_wmod"))], axis=1),
        "l0_wqk": halves(np.concatenate([pairs(f("L0_attn_W_q")), pairs(f("L0_attn_W_k"))]).T),
        "l0_wv": halves(f("L0_attn_W_v").T),
        "l0_wo": halves(f("L0_attn_W_o").T),
        "w_router": halves(f("L0_ffn_w_router")),
        "w_gate_fc": np.concatenate([f("L0_ffn_w_gate").reshape(E0, KH, P, HID), f("L0_ffn_w_fc").reshape(E0, KH, P, HID)],
                                    axis=3).transpose(0, 2, 1, 3),
        "w_proj": f("L0_ffn_w_proj"),
        "l1_wqk": halves(np.concatenate([f("L1_attn_Wq"), f("L1_attn_Wk")]).T),
        "l1_wkv": halves(np.concatenate([f("L1_attn_Wk"), f("L1_attn_Wv")]).T),
        "l1_wo": halves(f("L1_attn_Wo").T),
        "w_qkv": halves(f("L1_ffn_W_qkv")),
        "b_qk": f("L1_ffn_b_qkv")[:2 * D].reshape(4, P).T,
        "b_v": np.broadcast_to(f("L1_ffn_b_qkv")[2 * D:], (P, D)),
        "w_gate1": halves(f("L1_ffn_W_gate")),
        "b_gate1": np.broadcast_to(f("L1_ffn_b_gate"), (P, E1)),
        "w_exp": halves(f("L1_ffn_W_experts").transpose(1, 0, 2).reshape(D, E1 * D)),
        "b_exp": f("L1_ffn_b_experts"),
        "ident": np.eye(P, dtype=np.float32),
        "triu": (pi[:, None] <= pi[None, :]).astype(np.float32),
        "iota": np.tile(np.arange(E0, dtype=np.float32), (P, 1)),
        "head_of": (pi[:, None] // HD == np.arange(NHH)[None, :]).astype(np.float32),
        "cos": np.cos(angle).astype(np.float32),
        "sin": np.sin(angle).astype(np.float32),
    }
    return {k: np.ascontiguousarray(v) for k, v in out.items()}


def kernel(**inputs):
    import concourse.bacc as _bacc
    from concourse.bass_utils import run_bass_kernel_spmd as _run

    nc = _bacc.Bacc("TRN2", target_bir_lowering=False, num_devices=1)
    arrays = host_layout({k: np.asarray(v) for k, v in inputs.items()})
    tensors = {name: nc.dram_tensor(f"in_{name}", a.shape, mybir.dt.from_np(a.dtype), kind="ExternalInput").ap()
               for name, a in arrays.items()}
    build_program(nc, tensors, nc.dram_tensor("out", [B * T, D], F32, kind="ExternalOutput").ap())
    r = _run(nc, [{f"in_{k}": v for k, v in arrays.items()}], core_ids=[0])
    return r.results[0]["out"].reshape(B, T, D)
```
